# Optimizing a Trainium2 kernel written in Bass

```python
import numpy as np
import jax
import jax.numpy as jnp

def _softmax(x, axis=-1):
    return jax.nn.softmax(x, axis=axis)

def _gelu(x):
    return jax.nn.gelu(x, approximate=True)

def _silu(x):
    return jax.nn.silu(x)

def _sigmoid(x):
    return jax.nn.sigmoid(x)

def _layernorm(x, axis=-1, eps=1e-05):
    m = jnp.mean(x, axis=axis, keepdims=True)
    v = jnp.var(x, axis=axis, keepdims=True)
    return (x - m) / jnp.sqrt(v + eps)

def _scatter_add(tgt, idx, src, axis=0):
    return tgt.at[idx].add(src)

def _segment_sum(src, seg, n):
    return jax.ops.segment_sum(src, seg, n)
kernel_name = 'mk_gnn_resnorm_d4_gnn_r8_dd0937'

def setup_inputs(seed: int=0):
    np.random.seed(seed)
    _w = jnp.asarray

    def _rec_inputs():
        import jax
        import jax.numpy as jnp
        _gk = jax.random.key(seed)
        x = -0.000929 + 1 * jax.random.normal(jax.random.fold_in(_gk, 1), (8192, 16), jnp.float32)
        src = jax.random.randint(jax.random.fold_in(_gk, 2), (262144,), 0, 8192, jnp.int32)
        dst = jax.random.randint(jax.random.fold_in(_gk, 3), (262144,), 0, 8192, jnp.int32)
        _o = jnp.argsort(dst, stable=True)
        src = src[_o]
        dst = dst[_o]
        edge_attr_9 = 0.00033621 + 0.999798 * jax.random.normal(jax.random.fold_in(_gk, 11), (262144, 9), jnp.float32)
        edge_type_8 = jax.random.randint(jax.random.fold_in(_gk, 13), (262144,), 0, 8, jnp.int32)
        return (x, src, dst, edge_attr_9, edge_type_8)
    x, src, dst, edge_attr_9, edge_type_8 = _rec_inputs()

    def _L0_gnn_setup():
        import jax, jax.numpy as jnp
        import numpy as np
        N = 8192
        E = 131072
        NT = 4
        USERS = 8
        NUM_LAYERS = 3

        def _lin_init(k, fan_in, fan_out):
            bound = 1.0 / np.sqrt(fan_in)
            kw, kb = jax.random.split(k)
            W = jax.random.uniform(kw, (fan_in, fan_out), jnp.float32, -bound, bound)
            b = jax.random.uniform(kb, (fan_out,), jnp.float32, -bound, bound)
            return (W, b)

        def _igconv(x, edge_index, edge_attr, W1, b1, W2, b2, W3, b3, W4, b4):
            src, dst = (edge_index[0], edge_index[1])
            msg_in = jnp.concatenate([x[src], edge_attr], axis=1)
            h = jax.nn.relu(msg_in @ W1 + b1)
            msg = jax.nn.relu(h @ W2 + b2)
            aggr = jax.ops.segment_max(msg, dst, num_segments=N)
            aggr = jnp.where(jnp.isneginf(aggr), 0.0, aggr)
            tmp = jnp.concatenate([x, aggr], axis=1)
            h2 = jax.nn.relu(tmp @ W3 + b3)
            comb_all = h2 @ W4 + b4
            links = comb_all[:, 0:1]
            delay = comb_all[:, 1:2]
            comb = comb_all[:, 2:2 + 2 * NT]
            g = comb.reshape(-1, USERS, 2 * NT)
            ss = jnp.sum(g * g, axis=(1, 2), keepdims=True) + 1e-06
            comb = (g / jnp.sqrt(ss)).reshape(N, 2 * NT)
            return jnp.concatenate([links, delay, comb, x[:, :2 * NT - 2]], axis=1)
        key = jax.random.key(seed)
        ks = jax.random.split(key, 8)
        d_x = 4 * NT
        d_e = 2 * NT + 1
        x = jax.random.normal(ks[0], (N, d_x), jnp.float32)
        edge_index = jax.random.randint(ks[1], (2, E), 0, N, dtype=jnp.int32)
        edge_attr = jax.random.normal(ks[2], (E, d_e), jnp.float32)
        weights = jnp.ones((NUM_LAYERS,), jnp.int32)
        W1, b1 = _lin_init(ks[3], 6 * NT + 1, 64)
        W2, b2 = _lin_init(ks[4], 64, 64)
        W3, b3 = _lin_init(ks[5], 64 + 4 * NT, 32)
        W4, b4 = _lin_init(ks[6], 32, 2 + 2 * NT)
        return dict(x=x, edge_index=edge_index, edge_attr=edge_attr, weights=weights, W1=W1, b1=b1, W2=W2, b2=b2, W3=W3, b3=b3, W4=W4, b4=b4)
    _L0_gnn_all = _L0_gnn_setup()
    _L0_gnn_in = {k: v for k, v in _L0_gnn_all.items() if k in ('weights', 'W1', 'b1', 'W2', 'b2', 'W3', 'b3', 'W4', 'b4')}
    del _L0_gnn_all

    def _L1_gnn_setup():
        import jax, jax.numpy as jnp
        import numpy as np
        N_NODES = 12500
        N_EDGES = 400000
        FEAT = 16
        HID = 64
        key = jax.random.key(seed)
        ks = jax.random.split(key, 8)
        x = jax.random.normal(ks[0], (N_NODES, FEAT), dtype=jnp.float32)
        edge_index = jax.random.randint(ks[1], (2, N_EDGES), 0, N_NODES, dtype=jnp.int64)
        W1 = jax.random.normal(ks[2], (FEAT, HID), dtype=jnp.float32) * (1.0 / np.sqrt(FEAT))
        b1 = jax.random.normal(ks[3], (HID,), dtype=jnp.float32) * 0.01
        W2 = jax.random.normal(ks[4], (HID, HID), dtype=jnp.float32) * (1.0 / np.sqrt(HID))
        b2 = jax.random.normal(ks[5], (HID,), dtype=jnp.float32) * 0.01
        W3 = jax.random.normal(ks[6], (HID, FEAT), dtype=jnp.float32) * (1.0 / np.sqrt(HID))
        b3 = jax.random.normal(ks[7], (FEAT,), dtype=jnp.float32) * 0.01
        return {'x': x, 'edge_index': edge_index, 'W1': W1, 'b1': b1, 'W2': W2, 'b2': b2, 'W3': W3, 'b3': b3}
    _L1_gnn_all = _L1_gnn_setup()
    _L1_gnn_in = {k: v for k, v in _L1_gnn_all.items() if k in ('W1', 'b1', 'W2', 'b2', 'W3', 'b3')}
    del _L1_gnn_all

    def _L2_gnn_setup():
        import jax, jax.numpy as jnp
        import numpy as np
        N_NODES = 12500
        N_EDGES = 400000
        NUM_REL = 8

        def _rgcn_layer(x, src, dst, edge_type, W, root, bias):
            out = x @ root + bias
            x_src = x[src]
            for r in range(W.shape[0]):
                mask = (edge_type == r).astype(x.dtype)
                s = jax.ops.segment_sum(x_src * mask[:, None], dst, num_segments=x.shape[0])
                cnt = jax.ops.segment_sum(mask, dst, num_segments=x.shape[0])
                agg = s / jnp.clip(cnt, 1.0)[:, None]
                out = out + agg @ W[r]
            return out
        key = jax.random.key(seed)
        ks = jax.random.split(key, 9)
        x = jax.random.normal(ks[0], (N_NODES, 16), dtype=jnp.float32)
        edge_index = jax.random.randint(ks[1], (2, N_EDGES), 0, N_NODES, dtype=jnp.int32)
        edge_type = jax.random.randint(ks[2], (N_EDGES,), 0, NUM_REL, dtype=jnp.int32)
        s1 = 1.0 / np.sqrt(16.0)
        s2 = 1.0 / np.sqrt(32.0)
        W1 = jax.random.normal(ks[3], (NUM_REL, 16, 32), dtype=jnp.float32) * s1
        root1 = jax.random.normal(ks[4], (16, 32), dtype=jnp.float32) * s1
        b1 = jnp.zeros((32,), dtype=jnp.float32)
        W2 = jax.random.normal(ks[5], (NUM_REL, 32, 16), dtype=jnp.float32) * s2
        root2 = jax.random.normal(ks[6], (32, 16), dtype=jnp.float32) * s2
        b2 = jnp.zeros((16,), dtype=jnp.float32)
        return {'x': x, 'edge_index': edge_index, 'edge_type': edge_type, 'W1': W1, 'root1': root1, 'b1': b1, 'W2': W2, 'root2': root2, 'b2': b2}
    _L2_gnn_all = _L2_gnn_setup()
    _L2_gnn_in = {k: v for k, v in _L2_gnn_all.items() if k in ('W1', 'root1', 'b1', 'W2', 'root2', 'b2')}
    del _L2_gnn_all

    def _L3_gnn_setup():
        import jax, jax.numpy as jnp
        import numpy as np
        STALK_DIM = 16
        N_NODES = 6250
        N_EDGES = 50000
        HIDDEN = 64
        key = jax.random.key(seed)
        k1, k2, k3, k4 = jax.random.split(key, 4)
        d = STALK_DIM
        x = jax.random.normal(k1, (N_NODES, d), dtype=jnp.float32)
        edge_index = jax.random.randint(k2, (2, N_EDGES), 0, N_NODES, dtype=jnp.int64)
        W1 = jax.random.normal(k3, (HIDDEN, 2 * d), dtype=jnp.float32) * (1.0 / np.sqrt(2 * d))
        b1 = jnp.zeros((HIDDEN,), dtype=jnp.float32)
        W2 = jax.random.normal(k4, (d, HIDDEN), dtype=jnp.float32) * (1.0 / np.sqrt(HIDDEN))
        b2 = jnp.zeros((d,), dtype=jnp.float32)
        return {'x': x, 'edge_index': edge_index, 'W1': W1, 'b1': b1, 'W2': W2, 'b2': b2}
    _L3_gnn_all = _L3_gnn_setup()
    _L3_gnn_in = {k: v for k, v in _L3_gnn_all.items() if k in ('W1', 'b1', 'W2', 'b2')}
    del _L3_gnn_all
    return {'x': x, 'src': src, 'dst': dst, 'edge_attr_9': edge_attr_9, 'edge_type_8': edge_type_8, 'L0_gnn_weights': _L0_gnn_in['weights'], 'L0_gnn_W1': _L0_gnn_in['W1'], 'L0_gnn_b1': _L0_gnn_in['b1'], 'L0_gnn_W2': _L0_gnn_in['W2'], 'L0_gnn_b2': _L0_gnn_in['b2'], 'L0_gnn_W3': _L0_gnn_in['W3'], 'L0_gnn_b3': _L0_gnn_in['b3'], 'L0_gnn_W4': _L0_gnn_in['W4'], 'L0_gnn_b4': _L0_gnn_in['b4'], 'L1_gnn_W1': _L1_gnn_in['W1'], 'L1_gnn_b1': _L1_gnn_in['b1'], 'L1_gnn_W2': _L1_gnn_in['W2'], 'L1_gnn_b2': _L1_gnn_in['b2'], 'L1_gnn_W3': _L1_gnn_in['W3'], 'L1_gnn_b3': _L1_gnn_in['b3'], 'L2_gnn_W1': _L2_gnn_in['W1'], 'L2_gnn_root1': _L2_gnn_in['root1'], 'L2_gnn_b1': _L2_gnn_in['b1'], 'L2_gnn_W2': _L2_gnn_in['W2'], 'L2_gnn_root2': _L2_gnn_in['root2'], 'L2_gnn_b2': _L2_gnn_in['b2'], 'L3_gnn_W1': _L3_gnn_in['W1'], 'L3_gnn_b1': _L3_gnn_in['b1'], 'L3_gnn_W2': _L3_gnn_in['W2'], 'L3_gnn_b2': _L3_gnn_in['b2']}

def reference(x, src, dst, edge_attr_9, edge_type_8, L0_gnn_weights, L0_gnn_W1, L0_gnn_b1, L0_gnn_W2, L0_gnn_b2, L0_gnn_W3, L0_gnn_b3, L0_gnn_W4, L0_gnn_b4, L1_gnn_W1, L1_gnn_b1, L1_gnn_W2, L1_gnn_b2, L1_gnn_W3, L1_gnn_b3, L2_gnn_W1, L2_gnn_root1, L2_gnn_b1, L2_gnn_W2, L2_gnn_root2, L2_gnn_b2, L3_gnn_W1, L3_gnn_b1, L3_gnn_W2, L3_gnn_b2):
    import jax
    import jax.numpy as jnp

    def _L0_gnn_ref(x, edge_index, edge_attr, weights, W1, b1, W2, b2, W3, b3, W4, b4):
        import jax, jax.numpy as jnp
        import numpy as np
        N = 8192
        E = 131072
        NT = 4
        USERS = 8
        NUM_LAYERS = 3

        def _lin_init(k, fan_in, fan_out):
            bound = 1.0 / np.sqrt(fan_in)
            kw, kb = jax.random.split(k)
            W = jax.random.uniform(kw, (fan_in, fan_out), jnp.float32, -bound, bound)
            b = jax.random.uniform(kb, (fan_out,), jnp.float32, -bound, bound)
            return (W, b)

        def _igconv(x, edge_index, edge_attr, W1, b1, W2, b2, W3, b3, W4, b4):
            src, dst = (edge_index[0], edge_index[1])
            msg_in = jnp.concatenate([x[src], edge_attr], axis=1)
            h = jax.nn.relu(msg_in @ W1 + b1)
            msg = jax.nn.relu(h @ W2 + b2)
            aggr = jax.ops.segment_max(msg, dst, num_segments=N)
            aggr = jnp.where(jnp.isneginf(aggr), 0.0, aggr)
            tmp = jnp.concatenate([x, aggr], axis=1)
            h2 = jax.nn.relu(tmp @ W3 + b3)
            comb_all = h2 @ W4 + b4
            links = comb_all[:, 0:1]
            delay = comb_all[:, 1:2]
            comb = comb_all[:, 2:2 + 2 * NT]
            g = comb.reshape(-1, USERS, 2 * NT)
            ss = jnp.sum(g * g, axis=(1, 2), keepdims=True) + 1e-06
            comb = (g / jnp.sqrt(ss)).reshape(N, 2 * NT)
            return jnp.concatenate([links, delay, comb, x[:, :2 * NT - 2]], axis=1)
        x0 = x
        for i in range(NUM_LAYERS):
            y = _igconv(x0, edge_index, edge_attr, W1, b1, W2, b2, W3, b3, W4, b4)
            x0 = jnp.where(weights[i] > 0, y, x0)
        return x0

    def _L1_gnn_ref(x, edge_index, W1, b1, W2, b2, W3, b3):
        import jax, jax.numpy as jnp
        import numpy as np
        N_NODES = 12500
        N_EDGES = 400000
        FEAT = 16
        HID = 64
        N = x.shape[0]
        loops = jnp.arange(N, dtype=edge_index.dtype)
        row = jnp.concatenate([edge_index[0], loops])
        col = jnp.concatenate([edge_index[1], loops])
        deg = jax.ops.segment_sum(jnp.ones_like(col, dtype=x.dtype), col, num_segments=N)
        deg_inv_sqrt = jnp.where(deg > 0, jax.lax.rsqrt(jnp.maximum(deg, 1e-12)), 0.0)
        norm = deg_inv_sqrt[row] * deg_inv_sqrt[col]

        def gcn_layer(h, W, b):
            h = h @ W
            msg = norm[:, None] * h[row]
            agg = jax.ops.segment_sum(msg, col, num_segments=N)
            return agg + b
        h = jax.nn.relu(gcn_layer(x, W1, b1))
        h = jax.nn.relu(gcn_layer(h, W2, b2))
        return gcn_layer(h, W3, b3)

    def _L2_gnn_ref(x, edge_index, edge_type, W1, root1, b1, W2, root2, b2):
        import jax, jax.numpy as jnp
        import numpy as np
        N_NODES = 12500
        N_EDGES = 400000
        NUM_REL = 8

        def _rgcn_layer(x, src, dst, edge_type, W, root, bias):
            out = x @ root + bias
            x_src = x[src]
            for r in range(W.shape[0]):
                mask = (edge_type == r).astype(x.dtype)
                s = jax.ops.segment_sum(x_src * mask[:, None], dst, num_segments=x.shape[0])
                cnt = jax.ops.segment_sum(mask, dst, num_segments=x.shape[0])
                agg = s / jnp.clip(cnt, 1.0)[:, None]
                out = out + agg @ W[r]
            return out
        src, dst = (edge_index[0], edge_index[1])
        h = _rgcn_layer(x, src, dst, edge_type, W1, root1, b1)
        h = jax.nn.relu(h)
        h = _rgcn_layer(h, src, dst, edge_type, W2, root2, b2)
        return h

    def _L3_gnn_ref(x, edge_index, W1, b1, W2, b2):
        import jax, jax.numpy as jnp
        import numpy as np
        STALK_DIM = 16
        N_NODES = 6250
        N_EDGES = 50000
        HIDDEN = 64
        d = x.shape[1]
        n = x.shape[0]
        src, dst = (edge_index[0], edge_index[1])
        xs, xd = (x[src], x[dst])

        def reflection(a, b):
            h = jax.nn.relu(jnp.concatenate([a, b], axis=1) @ W1.T + b1)
            return h @ W2.T + b2

        def householder(v):
            vn = v / jnp.maximum(jnp.linalg.norm(v, axis=1, keepdims=True), 1e-12)
            return jnp.eye(d, dtype=v.dtype)[None] - 2.0 * vn[:, :, None] * vn[:, None, :]
        F_s = householder(reflection(xs, xd))
        F_d = householder(reflection(xd, xs))
        L_sd = -jnp.einsum('eki,ekj->eij', F_s, F_d)
        ones_e = jnp.ones(src.shape[0], dtype=x.dtype)
        deg = jnp.zeros(n, dtype=x.dtype).at[src].add(ones_e).at[dst].add(ones_e)
        deg_inv_sqrt = 1.0 / jnp.sqrt(jnp.maximum(deg, 1e-05))
        coef = deg_inv_sqrt[src] * deg_inv_sqrt[dst]
        msg_s = coef[:, None] * jnp.einsum('eij,ej->ei', L_sd, xd)
        msg_d = coef[:, None] * jnp.einsum('eji,ej->ei', L_sd, xs)
        out = x - jnp.zeros_like(x).at[src].add(msg_s) - jnp.zeros_like(x).at[dst].add(msg_d)
        return jax.nn.relu(out)
    edge_index = jnp.stack([src, dst])
    x = _layernorm(x + _L0_gnn_ref(x, edge_index, edge_attr_9, L0_gnn_weights, L0_gnn_W1, L0_gnn_b1, L0_gnn_W2, L0_gnn_b2, L0_gnn_W3, L0_gnn_b3, L0_gnn_W4, L0_gnn_b4), axis=-1)
    x = _layernorm(x + _L1_gnn_ref(x, edge_index, L1_gnn_W1, L1_gnn_b1, L1_gnn_W2, L1_gnn_b2, L1_gnn_W3, L1_gnn_b3), axis=-1)
    x = _layernorm(x + _L2_gnn_ref(x, edge_index, edge_type_8, L2_gnn_W1, L2_gnn_root1, L2_gnn_b1, L2_gnn_W2, L2_gnn_root2, L2_gnn_b2), axis=-1)
    x = _layernorm(x + _L3_gnn_ref(x, edge_index, L3_gnn_W1, L3_gnn_b1, L3_gnn_W2, L3_gnn_b2), axis=-1)
    return x

_drawn_inputs = setup_inputs


def setup_inputs(seed=0):
    import zlib

    import numpy as np

    out = dict(_drawn_inputs(seed))
    spreads = {'L2_gnn_b1': (0.0, 0.1),
     'L2_gnn_b2': (0.0, 0.1),
     'L3_gnn_b1': (0.0, 0.52),
     'L3_gnn_b2': (0.0, 0.311)}
    factors = {'edge_attr_9': 3.974, 'L1_gnn_b1': 5.299, 'L1_gnn_b2': 3.294, 'L0_gnn_b1': 3.725}
    for name, (base, spread) in spreads.items():
        noise = np.random.default_rng([zlib.crc32(name.encode()), seed]).standard_normal(out[name].shape)
        drawn = base * np.exp(spread * noise) if base else spread * noise
        out[name] = jnp.asarray(drawn.astype(out[name].dtype))
    for name, factor in factors.items():
        out[name] = (out[name] * factor).astype(out[name].dtype)
    return out
```

```python
import concourse.bass as bass
from concourse import mybir
from contextlib import ExitStack
import numpy as np


def gnn_stack_kernel(
    nc, x, src, dst, edge_attr, edge_type, L0_weights, L0_W1, L0_b1, L0_W2, L0_b2, L0_W3, L0_b3, L0_W4, L0_b4,
    L1_W1, L1_b1, L1_W2, L1_b2, L1_W3, L1_b3, L2_W1, L2_root1, L2_b1, L2_W2, L2_root2, L2_b2,
    L3_W1T, L3_b1, L3_W2T, L3_b2, out,
):
    fp32, bf16, fp16, i32 = mybir.dt.float32, mybir.dt.bfloat16, mybir.dt.float16, mybir.dt.int32
    ALU = mybir.AluOpType
    ACT = mybir.ActivationFunctionType
    AX = mybir.AxisListType.X

    P = 128
    N, D = x.shape
    E = src.shape[0]
    EP = E // P
    NT = N // P
    R, _, D2 = L2_W1.shape
    DA = edge_attr.shape[1]
    H = L0_W1.shape[1]
    H3 = L0_W3.shape[1]
    C4 = L0_W4.shape[1]
    USERS = 8
    LAYERS = L0_weights.shape[0]
    J = 64
    NC = EP // J
    SUB = 16
    GP = 4
    BIG = 3.0e38
    assert P * EP == E and P * NT == N and NC % 2 == 0

    ctx = ExitStack()

    def dram(name, shape, dt=fp32):
        return nc.dram_tensor(name, shape, dt).ap()

    t_table = dram("t_table", (N, D))
    t_table64 = dram("t_table64", (N, H))
    t_rel1 = dram("t_rel1", (N * R, D2))
    t_rel2 = dram("t_rel2", (N * R, D))
    t_inv8 = dram("t_inv8", (N, R))
    t_xdeg = dram("t_xdeg", (N, D + 1))
    S16 = dram("S16", (E + P, D))
    S32 = dram("S32", (E + P, D2))
    S64 = dram("S64", (E + P, H))
    X8 = dram("X8", (E + N, R))
    X17 = dram("X17", (E + N, D + 1))
    idx_rel = dram("idx_rel", (E,), i32)
    hi8_d = dram("hi8_d", (E,))
    lo8_d = dram("lo8_d", (E,))
    by_src = dram("by_src", (N, D))

    srcv = src.rearrange("(p j) -> p j", p=P)
    dstv = dst.rearrange("(p j) -> p j", p=P)
    typv = edge_type.rearrange("(p j) -> p j", p=P)
    relv = idx_rel.rearrange("(p j) -> p j", p=P)
    hi8v = hi8_d.rearrange("(p j) -> p j", p=P)
    lo8v = lo8_d.rearrange("(p j) -> p j", p=P)
    attrv = edge_attr.rearrange("(p j) f -> p (j f)", p=P)

    def edge_rows(t):
        return t[0:E, :].rearrange("(p j) f -> p (j f)", p=P)

    def node_rows(t):
        return t.rearrange("(p t) f -> p (t f)", p=P)

    def sb(c, name, shape, dt=fp32):
        return c.enter_context(nc.sbuf_tensor(name, shape, dt))

    def ps(c, name, shape, dt=fp32):
        return c.enter_context(nc.psum_tensor(name, shape, dt))

    class Phase(ExitStack):

        def __init__(self, tag):
            super().__init__()
            self.tag, self.sems = tag, []

        def sem(self, name):
            s = self.enter_context(nc.semaphore(f"{self.tag}_{name}"))
            self.sems.append(s)
            return s

        def sb(self, name, shape, dt=fp32):
            return sb(self, f"{self.tag}_{name}", shape, dt)

        def ps(self, name, shape, dt=fp32):
            return ps(self, f"{self.tag}_{name}", shape, dt)

        def close_block(self):
            nc.gpsimd.dma_reset()
            for s in self.sems:
                nc.gpsimd.sem_clear(s)
            nc.all_engine_barrier()

    class Chain:

        def __init__(self, eng, sem, base=0):
            self.eng, self.sem, self.base, self.n = eng, sem, base, 0

        def __call__(self, ins):
            self.n += 1
            ins.then_inc(self.sem, 1)

        def wait(self):
            self.eng.wait_ge(self.sem, self.base + self.n)

        def link(self, ins):
            self(ins)
            self.wait()

    with ctx:
        ident = sb(ctx, "ident", [P, P])
        keep = sb(ctx, "keep", [P, EP])
        wE = sb(ctx, "wE", [P, EP])
        xN = sb(ctx, "xN", [P, NT, D])
        xR = sb(ctx, "xR", [P, NT, D])
        lastE = sb(ctx, "lastE", [P, NT], i32)
        firstE = sb(ctx, "firstE", [P, NT], i32)
        has = sb(ctx, "has", [P, NT])
        dis1 = sb(ctx, "dis1", [P, NT])
        dis3 = sb(ctx, "dis3", [P, NT])
        inv8 = sb(ctx, "inv8", [P, NT, R])
        fixE = sb(ctx, "fixE", [P, 1], i32)
        dst0 = sb(ctx, "dst0", [P, 1], i32)
        krow = sb(ctx, "krow", [H, P])
        wmask = sb(ctx, "wmask", [P, LAYERS], i32)

        def setup():
            with Phase("su") as ph:
                d_cur = ph.sb("d_cur", [P, EP], i32)
                d_prev = ph.sb("d_prev", [P, EP], i32)
                s_src = ph.sb("s_src", [P, EP], i32)
                s_typ = ph.sb("s_typ", [P, EP], i32)
                tmpi = ph.sb("tmpi", [P, EP], i32)
                tmpj = ph.sb("tmpj", [P, EP], i32)
                hiD = ph.sb("hiD", [P, EP])
                loD = ph.sb("loD", [P, EP])
                hiS = ph.sb("hiS", [P, EP])
                loS = ph.sb("loS", [P, EP])
                hiS2 = ph.sb("hiS2", [P, EP])
                loS2 = ph.sb("loS2", [P, EP])
                d_next = ph.sb("d_next", [P, 1], i32)
                iot = ph.sb("iot", [P, 512], fp16)
                iotf = ph.sb("iotf", [P, 512])
                zero = ph.sb("zero", [P, 512], bf16)
                zf = ph.sb("zf", [P, 2048])
                U = 16
                keys = ph.sb("keys", [P, 2, 4, U])
                ohDh = ph.sb("ohDh", [P, 4, P], bf16)
                ohDl = ph.sb("ohDl", [P, 4, 512], bf16)
                ohSh = ph.sb("ohSh", [P, 4, P], bf16)
                ohSl = ph.sb("ohSl", [P, 4, NT], bf16)
                psD = ph.ps("psD", [P, 512])
                psS = ph.ps("psS", [P, 512])
                psO = ph.ps("psO", [P, 512])
                ltri = ph.sb("ltri", [P, P])
                cnt8 = ph.sb("cnt8", [P, NT, R])
                cntd = ph.sb("cntd", [P, NT])
                cnts = ph.sb("cnts", [P, NT])
                cum = ph.sb("cum", [P, NT])
                ones = ph.sb("ones", [P, NT])
                offs = ph.sb("offs", [P, 1])
                a1 = ph.sb("a1", [P, NT])
                a2 = ph.sb("a2", [P, NT])
                dummy = ph.sb("dummy", [P, NT], i32)
                dummyf = ph.sb("dummyf", [P, NT])
                col = ph.sb("col", [P, 8])
                kcol = ph.sb("kcol", [P, H])
                pcol = ph.sb("pcol", [P, 1], i32)
                eq0 = ph.sb("eq0", [P, EP])
                wm = ph.sb("wm", [P, LAYERS], i32)
                s_ld = ph.sem("loaded")
                s_x = ph.sem("x")
                s_cst = ph.sem("constants")
                s_v = ph.sem("vector")
                s_z = ph.sem("zeros_stored")
                s_zf = ph.sem("zero_tile")
                s_idx = ph.sem("indices_ready")
                s_st = ph.sem("stored")
                s_key = ph.sem("keys")
                s_oh = ph.sem("onehots")
                s_mm = ph.sem("counted")
                s_off = ph.sem("offsets")
                s_tot = ph.sem("totals")
                s_sq = ph.sem("roots")
                s_sqin = ph.sem("root_inputs")
                block = ph.enter_context(nc.Block())

                @block.sync
                def _(sp):
                    sp.dma_start(d_cur[:, :], dstv).then_inc(s_ld, 16)
                    sp.dma_start(d_prev[:, 1:EP], dstv[:, 0:EP - 1]).then_inc(s_ld, 16)
                    sp.dma_start(d_prev[1:P, 0:1], dstv[0:P - 1, EP - 1:EP], allow_slow_non_contiguous=True).then_inc(s_ld, 16)
                    sp.wait_ge(s_v, 2)
                    sp.dma_start(d_next[0:P - 1, 0:1], dstv[1:P, 0:1], allow_slow_non_contiguous=True).then_inc(s_ld, 16)
                    sp.dma_start(s_src[:, :], srcv).then_inc(s_ld, 16)
                    sp.dma_start(s_typ[:, :], typv).then_inc(s_ld, 16)
                    sp.dma_start(wm[:, :], L0_weights.rearrange("(a l) -> a l", a=1).broadcast_to([P, LAYERS])).then_inc(s_ld, 16)
                    sp.dma_start(xN[:, :, :].rearrange("p t f -> p (t f)"), node_rows(x)).then_inc(s_x, 16)
                    sp.dma_start(xR[:, :, :].rearrange("p t f -> p (t f)"), node_rows(x)).then_inc(s_x, 16)
                    sp.dma_start(t_table, x).then_inc(s_x, 16)
                    sp.wait_ge(s_idx, 1)
                    sp.dma_start(relv, tmpj[:, :]).then_inc(s_st, 16)
                    sp.wait_ge(s_idx, 2)
                    sp.dma_start(hi8v, hiS[:, :]).then_inc(s_st, 16)
                    sp.dma_start(lo8v, loS[:, :]).then_inc(s_st, 16)
                    sp.wait_ge(s_x, 48)
                    sp.wait_ge(s_idx, 3)
                    sp.dma_start(node_rows(t_inv8), inv8[:, :, :].rearrange("p t r -> p (t r)")).then_inc(s_st, 16)
                    sp.wait_ge(s_st, 64)

                @block.scalar
                def _(act):
                    act.wait_ge(s_zf, 1)
                    zw = zf.shape[1]
                    for buf, w in ((X8, R), (X17, D + 1)):
                        flat = buf[0:E, :].rearrange("(p j) f -> p (j f)", p=P)
                        for o in range(0, EP * w, zw):
                            act.dma_start(flat[:, o:o + zw], zf[:, :]).then_inc(s_z, 16)
                    for buf, w in ((S16, D), (S32, D2), (S64, H)):
                        act.dma_start(buf[E:E + P, :], zf[:, 0:w]).then_inc(s_z, 16)
                    n_zero = (EP * R + EP * (D + 1)) // zw + 3
                    act.wait_ge(s_idx, 2)
                    with act.Fori(0, EP // (2 * U)) as i:
                        for b in range(2):
                            act.wait_ge(s_oh, i * (8 * U) + 4 * U * b + 1)
                            act.wait_ge(s_idx, 2)
                            for k, t in enumerate((hiD, loD, hiS2, loS2)):
                                act.copy(keys[:, b, k, :], t[:, bass.ds(i * (2 * U) + b * U, U)]).then_inc(s_key, 1)
                    act.wait_ge(s_z, 16 * n_zero)
                    act.wait_ge(s_sqin, 1)
                    act.activation(a1[:, :], a1[:, :], ACT.Sqrt).then_inc(s_sq, 1)
                    act.activation(a2[:, :], a2[:, :], ACT.Sqrt).then_inc(s_sq, 1)

                @block.gpsimd
                def _(g):
                    g.memset(ident[:, :], 0.0).then_inc(s_cst, 1)
                    g.memset(ltri[:, :], 1.0).then_inc(s_cst, 1)
                    g.wait_ge(s_cst, 2)
                    g.affine_select(out=ident[:, :], in_=ident[:, :], compare_op=ALU.not_equal, fill=1.0,
                                    base=0, pattern=[[-1, P]], channel_multiplier=1).then_inc(s_cst, 1)
                    g.affine_select(out=ltri[:, :], in_=ltri[:, :], compare_op=ALU.is_ge, fill=0.0,
                                    base=-1, pattern=[[1, P]], channel_multiplier=-1).then_inc(s_cst, 1)
                    g.iota(iotf[:, :].bitcast(i32), pattern=[[1, 512]], base=0, channel_multiplier=0).then_inc(s_cst, 1)
                    g.iota(dummy[:, :], pattern=[[1, NT]], base=E, channel_multiplier=NT).then_inc(s_cst, 1)
                    g.iota(pcol[:, :], pattern=[[1, 1]], base=0, channel_multiplier=1).then_inc(s_cst, 1)

                @block.vector
                def _(v):
                    ch = Chain(v, s_v)
                    v.memset(zf[:, :], 0.0).then_inc(s_zf, 1)
                    ch(v.memset(d_prev[0:1, 0:1], -1))
                    ch(v.memset(d_next[:, :], -1))
                    ch(v.memset(zero[:, :], 0.0))
                    v.sem_inc(s_oh, 4 * U + 1)
                    ch(v.memset(ones[:, :], 1.0))
                    v.wait_ge(s_ld, 7 * 16)
                    v.wait_ge(s_cst, 7)
                    ch.wait()
                    ch.link(v.tensor_copy(iot[:, :], iotf[:, :].bitcast(i32)))
                    ch(v.tensor_copy(dummyf[:, :], dummy[:, :]))
                    ch(v.tensor_copy(dst0[:, :], d_cur[:, 0:1]))
                    ch(v.tensor_scalar(wmask[:, :], wm[:, :], 0.0, None, ALU.is_gt))
                    ch(v.tensor_tensor(keep[:, :], d_cur[:, :], d_prev[:, :], ALU.is_equal))
                    ch.link(v.tensor_scalar(tmpi[:, :], d_cur[:, :], 6, None, ALU.logical_shift_right))
                    ch.link(v.tensor_copy(hiD[:, :], tmpi[:, :]))
                    ch.link(v.tensor_scalar(tmpi[:, :], d_cur[:, :], NT - 1, None, ALU.bitwise_and))
                    ch.link(v.scalar_tensor_tensor(loD[:, :], tmpi[:, :], float(R), s_typ[:, :], ALU.mult, ALU.add))
                    ch.link(v.scalar_tensor_tensor(tmpj[:, :], s_src[:, :], float(R), s_typ[:, :], ALU.mult, ALU.add))
                    v.sem_inc(s_idx, 1)
                    ch.link(v.tensor_scalar(tmpi[:, :], s_src[:, :], 6, None, ALU.logical_shift_right))
                    ch.link(v.tensor_copy(hiS2[:, :], tmpi[:, :]))
                    ch.link(v.tensor_scalar(tmpi[:, :], s_src[:, :], NT - 1, None, ALU.bitwise_and))
                    ch.link(v.tensor_copy(loS2[:, :], tmpi[:, :]))
                    ch.link(v.tensor_scalar(tmpi[:, :], s_src[:, :], 3, None, ALU.logical_shift_right))
                    ch.link(v.tensor_copy(hiS[:, :], tmpi[:, :]))
                    ch.link(v.tensor_scalar(tmpi[:, :], s_src[:, :], 7, None, ALU.bitwise_and))
                    ch.link(v.tensor_copy(loS[:, :], tmpi[:, :]))
                    v.sem_inc(s_idx, 1)
                    ch.link(v.tensor_copy(col[:, 6:7], d_cur[:, 0:1]))
                    ch.link(v.tensor_scalar(eq0[:, :], d_cur[:, :], col[:, 6:7], None, ALU.is_equal))
                    ch(v.reduce_sum(col[:, 0:1], eq0[:, :], axis=AX))
                    ch(v.tensor_tensor(col[:, 1:2], d_cur[:, EP - 1:EP], d_next[:, :], ALU.is_equal))
                    ch(v.tensor_copy(col[:, 5:6], pcol[:, :]))
                    ch.wait()
                    ch.link(v.tensor_scalar(col[:, 2:3], col[:, 0:1], float(EP), None, ALU.is_equal))
                    ch.link(v.tensor_tensor(col[:, 2:3], col[:, 2:3], col[:, 1:2], ALU.mult))
                    ch.link(v.tensor_scalar(col[:, 2:3], col[:, 2:3], -1.0, 1.0, ALU.mult, ALU.add))
                    ch.link(v.tensor_tensor(col[:, 2:3], col[:, 2:3], keep[:, 0:1], ALU.mult))
                    ch.link(v.scalar_tensor_tensor(col[:, 3:4], col[:, 5:6], float(EP), col[:, 0:1], ALU.mult, ALU.add))
                    ch.link(v.tensor_scalar(col[:, 4:5], col[:, 5:6], float(E + 1), None, ALU.add))
                    ch.link(v.tensor_tensor(col[:, 3:4], col[:, 3:4], col[:, 4:5], ALU.subtract))
                    ch.link(v.tensor_tensor(col[:, 3:4], col[:, 3:4], col[:, 2:3], ALU.mult))
                    ch.link(v.scalar_tensor_tensor(fixE[:, :], col[:, 3:4], -1.0, col[:, 4:5], ALU.add, ALU.add))
                    ch.link(v.tensor_tensor(col[:, 7:8], d_cur[:, EP - 1:EP], d_prev[:, 0:1], ALU.is_equal))
                    v.tensor_copy(kcol[:, :], col[:, 7:8].broadcast_to([P, H])).then_inc(s_tot, 1)
                    with v.Fori(0, EP // (2 * U)) as i:
                        for b in range(2):
                            v.wait_ge(s_key, i * 8 + 4 * b + 4)
                            for u in range(U):
                                r = u % 4
                                m = i * (2 * U) + b * U + u
                                v.wait_ge(s_mm, m + 1)
                                v.tensor_scalar(ohDl[:, r, :], iot[:, :], keys[:, b, 1, u:u + 1], None, ALU.is_equal).then_inc(s_oh, 1)
                                v.tensor_scalar(ohDh[:, r, :], iot[:, 0:P], keys[:, b, 0, u:u + 1], None, ALU.is_equal).then_inc(s_oh, 1)
                                v.tensor_scalar(ohSl[:, r, :], iot[:, 0:NT], keys[:, b, 3, u:u + 1], None, ALU.is_equal).then_inc(s_oh, 1)
                                v.tensor_scalar(ohSh[:, r, :], iot[:, 0:P], keys[:, b, 2, u:u + 1], None, ALU.is_equal).then_inc(s_oh, 1)
                    v.wait_ge(s_mm, EP + 5)
                    ch(v.tensor_copy(cnt8[:, :, :].rearrange("p t r -> p (t r)"), psD[:, :]))
                    ch(v.tensor_copy(cnts[:, :], psS[:, 0:NT]))
                    ch.wait()
                    ch.link(v.reduce_sum(cntd[:, :], cnt8[:, :, :], axis=AX))
                    ch.link(v.tensor_tensor_scan(cum[:, :], ones[:, :], cntd[:, :], 0.0, ALU.mult, ALU.add))
                    v.tensor_copy(offs[:, :], cum[:, NT - 1:NT]).then_inc(s_tot, 1)
                    v.wait_ge(s_off, 2)
                    ch(v.tensor_copy(krow[:, :], psO[0:H, 0:P]))
                    ch(v.tensor_scalar(has[:, :], cntd[:, :], 0.5, None, ALU.is_gt))
                    ch.link(v.tensor_copy(col[:, 0:1], psO[:, 256:257]))
                    ch.link(v.tensor_scalar(cum[:, :], cum[:, :], col[:, 0:1], None, ALU.add))
                    ch.link(v.tensor_scalar(lastE[:, :], cum[:, :], -1.0, 0.0, ALU.add, ALU.max))
                    ch.link(v.tensor_tensor(cum[:, :], cum[:, :], cntd[:, :], ALU.subtract))
                    ch.link(v.tensor_tensor(cum[:, :], cum[:, :], dummyf[:, :], ALU.subtract))
                    ch.link(v.tensor_tensor(cum[:, :], cum[:, :], has[:, :], ALU.mult))
                    ch.link(v.tensor_tensor(firstE[:, :], cum[:, :], dummyf[:, :], ALU.add))
                    ch.link(v.tensor_scalar(cnt8[:, :, :], cnt8[:, :, :], 1.0, None, ALU.max))
                    ch.link(v.reciprocal(inv8[:, :, :], cnt8[:, :, :]))
                    v.sem_inc(s_idx, 1)
                    ch.link(v.tensor_scalar(a1[:, :], cntd[:, :], 1.0, None, ALU.add))
                    ch.link(v.tensor_tensor(a2[:, :], cntd[:, :], cnts[:, :], ALU.add))
                    ch.link(v.tensor_scalar(a2[:, :], a2[:, :], 1.0e-5, None, ALU.max))
                    v.sem_inc(s_sqin, 1)
                    v.wait_ge(s_sq, 2)
                    ch(v.reciprocal(dis1[:, :], a1[:, :]))
                    ch(v.reciprocal(dis3[:, :], a2[:, :]))
                    ch.wait()

                @block.tensor
                def _(pe):
                    pe.wait_ge(s_v, 4)
                    pe.sem_inc(s_mm, 4)
                    pe.matmul(psD[:, :], zero[:, 0:P], zero[:, :], start=True, stop=False, skip_group_check=True)
                    pe.matmul(psS[:, 0:NT], zero[:, 0:P], zero[:, 0:NT], start=True, stop=False, skip_group_check=True)
                    with pe.Fori(0, EP // 4) as i:
                        for r in range(4):
                            pe.wait_ge(s_oh, i * 16 + 4 * r + 5 + 4 * U)
                            pe.matmul(psD[:, :], ohDh[:, r, :], ohDl[:, r, :], start=False, stop=False, skip_group_check=True)
                            pe.matmul(psS[:, 0:NT], ohSh[:, r, :], ohSl[:, r, :], start=False, stop=False,
                                      skip_group_check=True).then_inc(s_mm, 1)
                    pe.matmul(psD[:, :], zero[:, 0:P], zero[:, :], start=False, stop=True, skip_group_check=True)
                    pe.matmul(psS[:, 0:NT], zero[:, 0:P], zero[:, 0:NT], start=False, stop=True, skip_group_check=True).then_inc(s_mm, 1)
                    pe.wait_ge(s_tot, 2)
                    pe.wait_ge(s_cst, 4)
                    pe.matmul(psO[0:H, 0:P], kcol[:, :], ident[:, :], start=True, stop=True).then_inc(s_off, 1)
                    pe.matmul(psO[:, 256:257], ltri[:, :], offs[:, :], start=True, stop=True).then_inc(s_off, 1)
            ph.close_block()

        def collect(tag, S, F, carry, G, is_max=False):
            with Phase(tag) as ph:
                lastT = ph.sb("lastT", [F, P])
                totT = ph.sb("totT", [F, P + 1])
                kop = ph.sb("kop", [F, P])
                tot = ph.sb("tot", [P, F])
                row = ph.sb("row", [P, F])
                psA = ph.ps("psA", [F, P])
                psB = ph.ps("psB", [P, F])
                s_t = ph.sem("transposed")
                s_v = ph.sem("vector")
                s_row = ph.sem("fix_rows")
                s_fix = ph.sem("fixed")
                s_g = ph.sem("gathered")
                block = ph.enter_context(nc.Block())

                @block.tensor
                def _(pe):
                    pe.transpose(psA[:, :], carry[:, :], ident[:, :]).then_inc(s_t, 1)
                    pe.wait_ge(s_v, 4)
                    pe.transpose(psB[:, :], totT[:, 0:P], ident[0:F, 0:F]).then_inc(s_t, 1)

                @block.vector
                def _(v):
                    ch = Chain(v, s_v)
                    if is_max:
                        ch(v.memset(totT[:, 0:1], -BIG))
                        ch(v.tensor_scalar(kop[:, :], krow[0:F, :], -1.0, BIG, ALU.add, ALU.mult))
                    else:
                        ch(v.memset(totT[:, 0:1], 0.0))
                        ch(v.tensor_copy(kop[:, :], krow[0:F, :]))
                    v.wait_ge(s_t, 1)
                    ch(v.tensor_copy(lastT[:, :], psA[:, :]))
                    ch.wait()
                    if is_max:
                        ch(v.tensor_tensor_scan(totT[:, 1:P + 1], kop[:, :], lastT[:, :], -BIG, ALU.add, ALU.max))
                    else:
                        ch(v.tensor_tensor_scan(totT[:, 1:P + 1], kop[:, :], lastT[:, :], 0.0, ALU.mult, ALU.add))
                    v.wait_ge(s_t, 2)
                    ch.link(v.tensor_copy(tot[:, :], psB[:, :]))
                    v.wait_ge(s_row, 16)
                    ch(v.tensor_tensor(row[:, :], row[:, :], tot[:, :], ALU.max if is_max else ALU.add))

                @block.gpsimd
                def _(g):
                    g.indirect_dma_start(out=row[:, :], out_offset=None, in_=S,
                                         in_offset=bass.IndirectOffsetOnAxis(ap=fixE[:, 0:1], axis=0)).then_inc(s_row, 16)
                    g.wait_ge(s_v, 6)
                    g.indirect_dma_start(out=S, out_offset=bass.IndirectOffsetOnAxis(ap=fixE[:, 0:1], axis=0),
                                         in_=row[:, :], in_offset=None).then_inc(s_fix, 16)
                    g.wait_ge(s_fix, 16)
                    for t in range(NT):
                        g.indirect_dma_start(out=G[:, t, :], out_offset=None, in_=S,
                                             in_offset=bass.IndirectOffsetOnAxis(ap=lastE[:, t:t + 1], axis=0)).then_inc(s_g, 16)
                    g.wait_ge(s_g, 16 * NT)
            ph.close_block()

        def sum_pass(tag, table, F, idxv, S, carry, weight=None):
            with Phase(tag) as ph:
                ix = ph.sb("ix", [P, 2, J], i32)
                G = ph.sb("G", [P, 2, J, F])
                kp = ph.sb("kp", [P, 2, J])
                wt = ph.sb("wt", [P, 2, J])
                s_ix = [ph.sem(f"index{b}") for b in range(2)]
                s_g = [ph.sem(f"gathered{b}") for b in range(2)]
                s_st = [ph.sem(f"stored{b}") for b in range(2)]
                s_free = ph.sem("slots_free")
                s_scan = ph.sem("scanned")
                s_v = ph.sem("vector")
                s_turn = ph.sem("turn")
                block = ph.enter_context(nc.Block())
                K = 4 if weight is not None else 2
                rows = edge_rows(S)

                @block.sync
                def _(sp):
                    sp.sem_inc(s_free, 2)
                    for b in range(2):
                        sp.dma_start(ix[:, b, :], idxv[:, b * J:(b + 1) * J]).then_inc(s_ix[b], 16)

                    def store(i, b):
                        sp.wait_ge(s_v, i * (2 * K) + K * (b + 1) + 1)
                        sp.dma_start(rows[:, bass.ds(i * (2 * J * F) + b * J * F, J * F)],
                                     G[:, b, :, :].rearrange("p j f -> p (j f)")).then_inc(s_st[b], 16)

                    with sp.Fori(0, NC // 2 - 1) as i:
                        for b in range(2):
                            store(i, b)
                            sp.wait_ge(s_st[b], i * 16 + 16)
                            sp.sem_inc(s_free, 1)
                            sp.dma_start(ix[:, b, :], idxv[:, bass.ds(i * (2 * J) + (2 + b) * J, J)]).then_inc(s_ix[b], 16)
                    for b in range(2):
                        c = NC - 2 + b
                        sp.wait_ge(s_v, K * (c + 1) + 1)
                        sp.dma_start(rows[:, c * J * F:(c + 1) * J * F],
                                     G[:, b, :, :].rearrange("p j f -> p (j f)")).then_inc(s_st[b], 16)
                    for b in range(2):
                        sp.wait_ge(s_st[b], 16 * (NC // 2))

                @block.gpsimd
                def _(g):
                    with g.Fori(0, NC // 2) as i:
                        for b in range(2):
                            g.wait_ge(s_ix[b], i * 16 + 16)
                            g.wait_ge(s_free, i * 2 + b + 1)
                            g.sem_inc(s_turn, 1)
                            for j in range(J):
                                g.indirect_dma_start(out=G[:, b, j, :], out_offset=None, in_=table,
                                                     in_offset=bass.IndirectOffsetOnAxis(ap=ix[:, b, j:j + 1], axis=0)).then_inc(s_g[b], 16)

                @block.vector
                def _(v):
                    v.memset(carry[:, :], 0.0).then_inc(s_v, 1)
                    with v.Fori(0, NC // 2) as i:
                        for b in range(2):
                            ch = Chain(v, s_v, i * (2 * K) + K * b + 1)
                            ch.wait()
                            ch(v.tensor_scalar(kp[:, b, :], keep[:, bass.ds(i * (2 * J) + b * J, J)], 1.0, None, ALU.mult))
                            if weight is not None:
                                ch(v.tensor_scalar(wt[:, b, :], weight[:, bass.ds(i * (2 * J) + b * J, J)], 1.0, None, ALU.mult))
                            v.wait_ge(s_g[b], i * (16 * J) + 16 * J)
                            ch.wait()
                            if weight is not None:
                                ch.link(v.tensor_tensor(G[:, b, :, :], G[:, b, :, :],
                                                        wt[:, b, :].unsqueeze(2).broadcast_to([P, J, F]), ALU.mult))
                            for f in range(F):
                                v.tensor_tensor_scan(G[:, b, :, f], kp[:, b, :], G[:, b, :, f], carry[:, f:f + 1],
                                                     ALU.mult, ALU.add).then_inc(s_scan, 1)
                            v.wait_ge(s_scan, i * (2 * F) + F * (b + 1))
                            ch(v.tensor_copy(carry[:, :], G[:, b, J - 1, :]))
                            assert ch.n == K
            ph.close_block()

        def message_pass(tag, W1b, W2b, carry):
            with Phase(tag) as ph:
                ix = ph.sb("ix", [P, 2, J], i32)
                ea = ph.sb("ea", [P, 2, J * DA])
                G = ph.sb("G", [P, 2, J, 32])
                M = ph.sb("M", [P, 2, J, H])
                pen = ph.sb("pen", [P, 2, J])
                XT = ph.sb("XT", [P, 2, 512])
                HT = ph.sb("HT", [P, 2, 512])
                psT = [ph.ps(f"psT{b}", [P, 512]) for b in range(2)]
                psH = [ph.ps(f"psH{b}", [P, 512]) for b in range(2)]
                psM = [ph.ps(f"psM{b}", [P, 1024]) for b in range(2)]
                s_ix = [ph.sem(f"index{b}") for b in range(2)]
                s_ea = [ph.sem(f"attr{b}") for b in range(2)]
                s_g = [ph.sem(f"gathered{b}") for b in range(2)]
                s_st = [ph.sem(f"stored{b}") for b in range(2)]
                s_row = ph.sem("rows_complete")
                s_t = ph.sem("transposed")
                s_xt = ph.sem("xt")
                s_m1 = ph.sem("hidden")
                s_h = ph.sem("relu")
                s_m2 = ph.sem("messages")
                s_ev = ph.sem("messages_out")
                s_scan = ph.sem("scanned")
                s_v = ph.sem("vector")
                s_free = ph.sem("slots_free")
                s_turn = ph.sem("turn")
                block = ph.enter_context(nc.Block())
                NS = J // SUB
                rows = edge_rows(S64)

                @block.sync
                def _(sp):
                    sp.sem_inc(s_free, 2)

                    def load(b, cols, acols):
                        sp.dma_start(ix[:, b, :], srcv[:, cols]).then_inc(s_ix[b], 16)
                        sp.dma_start(ea[:, b, :], attrv[:, acols]).then_inc(s_ea[b], 16)

                    for b in range(2):
                        load(b, slice(b * J, (b + 1) * J), slice(b * J * DA, (b + 1) * J * DA))
                    with sp.Fori(0, NC // 2 - 1) as i:
                        for b in range(2):
                            sp.wait_ge(s_v, i * 4 + 2 * b + 3)
                            sp.dma_start(rows[:, bass.ds(i * (2 * J * H) + b * J * H, J * H)],
                                         M[:, b, :, :].rearrange("p j f -> p (j f)")).then_inc(s_st[b], 16)
                            sp.wait_ge(s_st[b], i * 16 + 16)
                            sp.sem_inc(s_free, 1)
                            load(b, bass.ds(i * (2 * J) + (2 + b) * J, J),
                                 bass.ds(i * (2 * J * DA) + (2 + b) * J * DA, J * DA))
                    for b in range(2):
                        c = NC - 2 + b
                        sp.wait_ge(s_v, 2 * (c + 1) + 1)
                        sp.dma_start(rows[:, c * J * H:(c + 1) * J * H],
                                     M[:, b, :, :].rearrange("p j f -> p (j f)")).then_inc(s_st[b], 16)
                    for b in range(2):
                        sp.wait_ge(s_st[b], 16 * (NC // 2))

                @block.gpsimd
                def _(g):
                    for b in range(2):
                        g.memset(G[:, b, :, :], 0.0).then_inc(s_row, 1)
                    g.wait_ge(s_row, 2)
                    for b in range(2):
                        g.memset(G[:, b, :, D + DA:D + DA + 1], 1.0).then_inc(s_row, 1)
                    g.wait_ge(s_row, 4)
                    with g.Fori(0, NC // 2) as i:
                        for b in range(2):
                            g.wait_ge(s_ix[b], i * 16 + 16)
                            g.wait_ge(s_t, i * (2 * NS) + NS * (b + 1))
                            g.sem_inc(s_turn, 1)
                            for j in range(J):
                                g.indirect_dma_start(out=G[:, b, j, 0:D], out_offset=None, in_=t_table,
                                                     in_offset=bass.IndirectOffsetOnAxis(ap=ix[:, b, j:j + 1], axis=0)).then_inc(s_g[b], 16)

                @block.scalar
                def _(act):
                    act.sem_inc(s_h, 1)
                    act.wait_ge(s_row, 4)
                    with act.Fori(0, NC // 2) as i:
                        for b in range(2):
                            act.wait_ge(s_ea[b], i * 16 + 16)
                            act.wait_ge(s_t, i * (2 * NS) + NS * (b + 1))
                            act.copy(G[:, b, :, D:D + DA], ea[:, b, :].rearrange("p (j f) -> p j f", f=DA)).then_inc(s_row, 1)
                            for s in range(NS):
                                n = b * NS + s
                                act.wait_ge(s_t, i * (2 * NS) + n + 1 + 2 * NS)
                                act.copy(XT[:, s % 2, :], psT[s % 2][:, :]).then_inc(s_xt, 1)
                                act.wait_ge(s_m1, i * (2 * NS) + n + 1)
                                act.wait_ge(s_m2, i * (2 * NS) + n + 1)
                                act.activation(HT[:, 0, :], psH[0][:, :], ACT.Relu).then_inc(s_h, 1)
                                act.activation(HT[:, 1, :], psH[1][:, :], ACT.Relu).then_inc(s_h, 1)
                                act.wait_ge(s_m2, i * (2 * NS) + n + 2)
                                if s == 0:
                                    act.wait_ge(s_free, i * 2 + b + 1)
                                act.copy(M[:, b, s * SUB:(s + 1) * SUB, :].rearrange("p j f -> p (j f)"),
                                         psM[s % 2][:, :]).then_inc(s_ev, 1)

                @block.tensor
                def _(pe):
                    pe.sem_inc(s_t, 2 * NS)
                    pe.sem_inc(s_m2, 1)
                    with pe.Fori(0, NC // 2) as i:
                        for b in range(2):
                            pe.wait_ge(s_g[b], i * (16 * J) + 16 * J)
                            pe.wait_ge(s_row, i * 2 + b + 5)
                            for s in range(NS):
                                n = b * NS + s
                                for q in range(4):
                                    o = s * SUB + 4 * q
                                    ins = pe.transpose(psT[s % 2][:, q * P:(q + 1) * P],
                                                       G[:, b, o:o + 4, :].rearrange("p j f -> p (j f)"), ident[:, :])
                                ins.then_inc(s_t, 1)
                                pe.wait_ge(s_xt, i * (2 * NS) + n + 1)
                                pe.wait_ge(s_h, i * (4 * NS) + 2 * n + 1)
                                for h in range(2):
                                    ins = pe.matmul(psH[h][:, :], W1b[64 * h:64 * h + 64, :], XT[64 * h:64 * h + 64, s % 2, :],
                                                    start=True, stop=True)
                                ins.then_inc(s_m1, 1)
                                pe.wait_ge(s_h, i * (4 * NS) + 2 * n + 3)
                                for q in range(4):
                                    for h in range(2):
                                        o = (4 * q + 2 * h) * H
                                        ins = pe.matmul(psM[s % 2][:, o:o + 2 * H], HT[:, h, q * P:(q + 1) * P], W2b[:, :],
                                                        start=True, stop=True)
                                ins.then_inc(s_m2, 1)

                @block.vector
                def _(v):
                    v.memset(carry[:, :], -BIG).then_inc(s_v, 1)
                    with v.Fori(0, NC // 2) as i:
                        for b in range(2):
                            ch = Chain(v, s_v, i * 4 + 2 * b + 1)
                            ch.wait()
                            ch(v.tensor_scalar(pen[:, b, :], keep[:, bass.ds(i * (2 * J) + b * J, J)], -1.0, BIG, ALU.add, ALU.mult))
                            v.wait_ge(s_ev, i * (2 * NS) + NS * (b + 1))
                            ch.wait()
                            for f in range(H):
                                v.tensor_tensor_scan(M[:, b, :, f], pen[:, b, :], M[:, b, :, f], carry[:, f:f + 1],
                                                     ALU.add, ALU.max).then_inc(s_scan, 1)
                            v.wait_ge(s_scan, i * (2 * H) + H * (b + 1))
                            ch(v.tensor_copy(carry[:, :], M[:, b, J - 1, :]))
            ph.close_block()

        def node_mlp(tag, X, Fi, Y, Fo, W2, W1=None, b1=None, Hd=None):
            with Phase(tag) as ph:
                NG = NT // GP
                Hd = Hd if W1 is not None else Fi
                bank = 512 if Fo > P else Fo
                xs = ph.sb("xs", [P, 2, GP, Fi])
                xt = ph.sb("xt", [Fi, 2, GP * P])
                ht = ph.sb("ht", [Hd, 2, GP * P])
                psX = ph.ps("psX", [Fi, GP * P])
                psH = ph.ps("psH", [Hd, GP * P])
                psY = ph.ps("psY", [P, GP, bank])
                s_x = ph.sem("staged")
                s_t = ph.sem("transposed")
                s_xt = ph.sem("xt")
                s_h = ph.sem("hidden")
                s_ht = ph.sem("relu")
                s_y = ph.sem("products")
                s_yo = ph.sem("out")
                s_turn = ph.sem("turn")
                s_turn2 = ph.sem("turn_out")
                block = ph.enter_context(nc.Block())
                src_t = ht if W1 is not None else xt

                @block.vector
                def _(v):
                    with v.Fori(0, NG // 2) as i:
                        for b in range(2):
                            v.tensor_scalar(xs[:, b, :, :], X[:, bass.ds(i * (2 * GP) + b * GP, GP), :], 1.0, None,
                                            ALU.mult).then_inc(s_x, 1)
                            v.wait_ge(s_t, i * 2 + b + 1)
                            v.wait_ge(s_y, i * 2 + b + 1)
                            if W1 is None and b1 is not None:
                                v.tensor_scalar(xt[:, b, :], psX[:, :], b1, 0.0, ALU.add, ALU.max).then_inc(s_xt, 1)
                            else:
                                v.tensor_copy(xt[:, b, :], psX[:, :]).then_inc(s_xt, 1)

                @block.scalar
                def _(act):
                    act.sem_inc(s_yo, 1)
                    with act.Fori(0, NG // 2) as i:
                        for b in range(2):
                            if W1 is not None:
                                act.wait_ge(s_h, i * 2 + b + 1)
                                act.activation(ht[:, b, :], psH[:, :], ACT.Relu, bias=b1).then_inc(s_ht, 1)
                            act.wait_ge(s_y, i * 2 + b + 2)
                            act.sem_inc(s_turn2, 1)
                            act.copy(Y[:, bass.ds(i * (2 * GP) + b * GP, GP), :], psY[:, :, 0:Fo]).then_inc(s_yo, 1)

                @block.tensor
                def _(pe):
                    pe.sem_inc(s_y, 1)
                    with pe.Fori(0, NG // 2) as i:
                        for b in range(2):
                            pe.wait_ge(s_x, i * 2 + b + 1)
                            pe.sem_inc(s_turn, 1)
                            for t in range(GP):
                                ins = pe.transpose(psX[:, t * P:(t + 1) * P], xs[:, b, t, :], ident[:, :])
                            ins.then_inc(s_t, 1)
                            pe.wait_ge(s_xt, i * 2 + b + 1)
                            if W1 is not None:
                                pe.matmul(psH[:, :], W1, xt[:, b, :], start=True, stop=True).then_inc(s_h, 1)
                                pe.wait_ge(s_ht, i * 2 + b + 1)
                            pe.wait_ge(s_yo, i * 2 + b + 1)
                            for t in range(GP):
                                ins = pe.matmul(psY[:, t, 0:Fo], src_t[:, b, t * P:(t + 1) * P], W2, start=True, stop=True)
                            ins.then_inc(s_y, 1)
            ph.close_block()

        def bcast(vec, n):
            return vec.rearrange("(a n) -> a n", a=1).broadcast_to([P, n])

        def column(vec):
            return vec.rearrange("(p a) -> p a", a=1)

        def over_f(t, F):
            return t.unsqueeze(2).broadcast_to([P, NT, F])

        def over_t(t, F):
            return t.unsqueeze(1).broadcast_to([P, NT, F])

        def steps(tag, body, loads=(), stores=()):
            with Phase(tag) as ph:
                s_ld = ph.sem("loaded")
                s_v = ph.sem("vector")
                s_done = ph.sem("values")
                s_st = ph.sem("stored")
                s_q = ph.sem("root_input")
                s_r = ph.sem("root")
                roots = []
                block = ph.enter_context(nc.Block())

                @block.vector
                def _(v):
                    ch = Chain(v, s_v)
                    if loads:
                        v.wait_ge(s_ld, 16 * len(loads))

                    def root(t):
                        roots.append(t)
                        v.sem_inc(s_q, 1)
                        v.wait_ge(s_r, len(roots))

                    body(v, ch, root, ph)
                    v.sem_inc(s_done, 1)

                @block.scalar
                def _(act):
                    for n, t in enumerate(roots):
                        act.wait_ge(s_q, n + 1)
                        act.activation(t, t, ACT.Sqrt).then_inc(s_r, 1)

                @block.sync
                def _(sp):
                    for o, i in loads:
                        sp.dma_start(o, i).then_inc(s_ld, 16)
                    if stores:
                        sp.wait_ge(s_done, 1)
                        for o, i in stores:
                            sp.dma_start(o, i).then_inc(s_st, 16)
                        sp.wait_ge(s_st, 16 * len(stores))
            ph.close_block()

        def norm_residual(v, ch, root, Z, m, var, sq):
            ch.link(v.tensor_tensor(Z, Z, xR[:, :, :], ALU.add))
            ch.link(v.reduce_sum(m, Z, axis=AX))
            ch.link(v.tensor_scalar(m, m, -1.0 / D, None, ALU.mult))
            ch.link(v.tensor_tensor(Z, Z, over_f(m, D), ALU.add))
            ch.link(v.tensor_tensor(sq, Z, Z, ALU.mult))
            ch.link(v.reduce_sum(var, sq, axis=AX))
            ch.link(v.tensor_scalar(var, var, 1.0 / D, 1.0e-5, ALU.mult, ALU.add))
            root(var)
            ch.link(v.reciprocal(m, var))
            ch.link(v.tensor_tensor(xN[:, :, :], Z, over_f(m, D), ALU.mult))
            ch.link(v.tensor_copy(xR[:, :, :], xN[:, :, :]))

        setup()

        flat = lambda t: t[:, :, :].rearrange("p t f -> p (t f)")

        with ExitStack() as c:
            W1b = sb(c, "W1b", [P, P])
            W2b = sb(c, "W2b", [P, P])
            W3s = sb(c, "W3s", [D + H, H3])
            b3s = sb(c, "b3s", [H3, 1])
            W4s = sb(c, "W4s", [H3, C4])
            b2n = sb(c, "b2n", [P, H])
            b4n = sb(c, "b4n", [P, C4])
            carry = sb(c, "carry0", [P, H])

            def clear(v, ch, root, ph):
                pass
            with Phase("w0") as ph:
                s_z = ph.sem("zeroed")
                s_w = ph.sem("weights")
                block = ph.enter_context(nc.Block())

                @block.vector
                def _(v):
                    v.memset(W1b[:, :], 0.0).then_inc(s_z, 1)
                    v.memset(W2b[:, :], 0.0).then_inc(s_z, 1)

                @block.sync
                def _(sp):
                    sp.wait_ge(s_z, 2)
                    n = 0
                    for q in range(4):
                        o = H * (q % 2)
                        sp.dma_start(W1b[32 * q:32 * q + D + DA, o:o + H], L0_W1).then_inc(s_w, 16)
                        sp.dma_start(W1b[32 * q + D + DA:32 * q + D + DA + 1, o:o + H],
                                     L0_b1.rearrange("(a n) -> a n", a=1)).then_inc(s_w, 16)
                        n += 2
                    for q in range(2):
                        sp.dma_start(W2b[H * q:H * q + H, H * q:H * q + H], L0_W2).then_inc(s_w, 16)
                    for o, i in ((W3s[:, :], L0_W3), (b3s[:, :], column(L0_b3)), (W4s[:, :], L0_W4),
                                 (b2n[:, :], bcast(L0_b2, H)), (b4n[:, :], bcast(L0_b4, C4))):
                        sp.dma_start(o, i).then_inc(s_w, 16)
                    sp.wait_ge(s_w, 16 * (n + 7))
            ph.close_block()

            with nc.Fori(0, LAYERS) as layer:
                message_pass("mp", W1b, W2b, carry)
                with ExitStack() as cc:
                    G = sb(cc, "Gn0", [P, NT, H])
                    X80 = sb(cc, "X80", [P, NT, D + H])
                    Y = sb(cc, "Y10", [P, NT, C4])
                    sq = sb(cc, "sq0", [P, NT, 8])
                    ss = sb(cc, "ss0", [P, NT // USERS])
                    ynew = sb(cc, "ynew", [P, NT, D])
                    wl = sb(cc, "wl", [P, 1], i32)
                    wfull = sb(cc, "wfull", [P, NT, D], i32)
                    collect("mc", S64, H, carry, G, is_max=True)

                    def aggregate(v, ch, root, ph):
                        ch(v.tensor_copy(X80[:, :, 0:D], xN[:, :, :]))
                        ch.link(v.tensor_tensor(G[:, :, :], G[:, :, :], over_t(b2n[:, :], H), ALU.add))
                        ch.link(v.scalar_tensor_tensor(X80[:, :, D:D + H], G[:, :, :], 0.0, over_f(has[:, :], H), ALU.max, ALU.mult))
                    steps("ma", aggregate)
                    node_mlp("mn", X80, D + H, Y, C4, W4s[:, :], W1=W3s[:, :], b1=b3s[:, 0:1], Hd=H3)

                    def select(v, ch, root, ph):
                        ch(v.tensor_copy(wl[:, :], wmask[:, bass.ds(layer, 1)]))
                        ch.link(v.tensor_tensor(Y[:, :, :], Y[:, :, :], over_t(b4n[:, :], C4), ALU.add))
                        ch(v.tensor_copy(wfull[:, :, :].rearrange("p t f -> p (t f)"), wl[:, :].broadcast_to([P, NT * D])))
                        ch.link(v.tensor_tensor(sq[:, :, :], Y[:, :, 2:C4], Y[:, :, 2:C4], ALU.mult))
                        ch.link(v.reduce_sum(ss[:, :], sq[:, :, :].rearrange("p (g u) f -> p g (u f)", u=USERS), axis=AX))
                        ch.link(v.tensor_scalar(ss[:, :], ss[:, :], 1.0e-6, None, ALU.add))
                        root(ss[:, :])
                        ch.link(v.reciprocal(ss[:, :], ss[:, :]))
                        ch(v.tensor_copy(ynew[:, :, 0:2], Y[:, :, 0:2]))
                        ch(v.tensor_copy(ynew[:, :, C4:D], xN[:, :, 0:D - C4]))
                        ch.link(v.tensor_tensor(ynew[:, :, 2:C4].rearrange("p (g u) f -> p g u f", u=USERS),
                                                Y[:, :, 2:C4].rearrange("p (g u) f -> p g u f", u=USERS),
                                                ss[:, :].unsqueeze(2).unsqueeze(3).broadcast_to([P, NT // USERS, USERS, 8]), ALU.mult))
                        ch.wait()
                        ch.link(v.copy_predicated(flat(xN), flat(wfull), flat(ynew)))
                    steps("ms", select, stores=[(node_rows(t_table), flat(xN))])

        with ExitStack() as c:
            zt = sb(c, "zt", [P, NT, D])
            sq = sb(c, "sqn", [P, NT, D])
            m = sb(c, "mn", [P, NT])
            var = sb(c, "var", [P, NT])
            ag = sb(c, "ag", [P, NT, D])
            tb = sb(c, "tb", [P, NT, D])
            carry = sb(c, "carry1", [P, D])
            W1s = sb(c, "W1s", [D, H])
            b1c = sb(c, "b1c", [H, 1])
            W2s = sb(c, "W2s", [H, H])
            b2c = sb(c, "b2c", [H, 1])
            W3t = sb(c, "W3t", [H, D])
            b3n = sb(c, "b3n", [P, D])

            def masked_sum(v, ch, G, F):
                ch.link(v.tensor_tensor(G[:, :, :], G[:, :, :], over_f(has[:, :], F), ALU.mult))

            def norm0(v, ch, root, ph):
                ch.link(v.tensor_copy(zt[:, :, :], xN[:, :, :]))
                norm_residual(v, ch, root, zt[:, :, :], m[:, :], var[:, :], sq[:, :, :])
                ch.link(v.tensor_tensor(tb[:, :, :], xN[:, :, :], over_f(dis1[:, :], D), ALU.mult))
            steps("n0", norm0, loads=[(W1s[:, :], L1_W1), (b1c[:, :], column(L1_b1)), (W2s[:, :], L1_W2),
                                      (b2c[:, :], column(L1_b2)), (W3t[:, :], L1_W3), (b3n[:, :], bcast(L1_b3, D))],
                  stores=[(node_rows(t_table), flat(tb))])

            sum_pass("p1", t_table, D, srcv, S16, carry)
            collect("c1", S16, D, carry, ag)

            def gather1(v, ch, root, ph):
                masked_sum(v, ch, ag, D)
                ch.link(v.tensor_tensor(ag[:, :, :], ag[:, :, :], tb[:, :, :], ALU.add))
                ch.link(v.tensor_tensor(ag[:, :, :], ag[:, :, :], over_f(dis1[:, :], D), ALU.mult))
            steps("a1", gather1)
            with ExitStack() as cc:
                h1 = sb(cc, "h1", [P, NT, H])
                g2 = sb(cc, "g2", [P, NT, H])
                carry64 = sb(cc, "carry2", [P, H])
                node_mlp("m1", ag, D, h1, H, W2s[:, :], W1=W1s[:, :], b1=b1c[:, 0:1], Hd=H)

                def scale1(v, ch, root, ph):
                    ch.link(v.tensor_tensor(h1[:, :, :], h1[:, :, :], over_f(dis1[:, :], H), ALU.mult))
                steps("s1", scale1, stores=[(node_rows(t_table64), flat(h1))])
                sum_pass("p2", t_table64, H, srcv, S64, carry64)
                collect("c2", S64, H, carry64, g2)

                def gather2(v, ch, root, ph):
                    masked_sum(v, ch, g2, H)
                    ch.link(v.tensor_tensor(g2[:, :, :], g2[:, :, :], h1[:, :, :], ALU.add))
                    ch.link(v.tensor_tensor(g2[:, :, :], g2[:, :, :], over_f(dis1[:, :], H), ALU.mult))
                steps("a2", gather2)
                node_mlp("m2", g2, H, tb, D, W3t[:, :], b1=b2c[:, 0:1])

            def scale2(v, ch, root, ph):
                ch.link(v.tensor_tensor(tb[:, :, :], tb[:, :, :], over_f(dis1[:, :], D), ALU.mult))
            steps("s2", scale2, stores=[(node_rows(t_table), flat(tb))])
            sum_pass("p3", t_table, D, srcv, S16, carry)
            collect("c3", S16, D, carry, ag)

            def gather3(v, ch, root, ph):
                masked_sum(v, ch, ag, D)
                ch.link(v.tensor_tensor(ag[:, :, :], ag[:, :, :], tb[:, :, :], ALU.add))
                ch.link(v.tensor_tensor(ag[:, :, :], ag[:, :, :], over_f(dis1[:, :], D), ALU.mult))
                ch.link(v.tensor_tensor(ag[:, :, :], ag[:, :, :], over_t(b3n[:, :], D), ALU.add))
                norm_residual(v, ch, root, ag[:, :, :], m[:, :], var[:, :], sq[:, :, :])
            steps("a3", gather3)

        def spread(tag, X, buf, table, first, F):
            with Phase(tag) as ph:
                s_s = ph.sem("scattered")
                s_f = ph.sem("first")
                block = ph.enter_context(nc.Block())

                @block.gpsimd
                def _(g):
                    for t in range(NT):
                        g.indirect_dma_start(out=buf, out_offset=bass.IndirectOffsetOnAxis(ap=firstE[:, t:t + 1], axis=0),
                                             in_=X[:, t, :], in_offset=None).then_inc(s_s, 16)
                    g.indirect_dma_start(out=first[:, :], out_offset=None, in_=table,
                                         in_offset=bass.IndirectOffsetOnAxis(ap=dst0[:, 0:1], axis=0)).then_inc(s_f, 16)
                    g.wait_ge(s_s, 16 * NT)
                    g.wait_ge(s_f, 16)
            ph.close_block()

        def edge_weights():
            with ExitStack() as c:
                first = sb(c, "first8", [P, R])
                spread("sp8", inv8, X8, t_inv8, first, R)
                rows = edge_rows(X8)
                with Phase("ew") as ph:
                    X = ph.sb("X", [P, 2, J, R])
                    ty = ph.sb("ty", [P, 2, J], i32)
                    kp = ph.sb("kp", [P, 2, J])
                    oh = ph.sb("oh", [P, J, R])
                    rel = ph.sb("rel", [P, R], i32)
                    s_x = [ph.sem(f"rows{b}") for b in range(2)]
                    s_ty = [ph.sem(f"types{b}") for b in range(2)]
                    s_v = ph.sem("vector")
                    s_c = ph.sem("constants")
                    s_scan = ph.sem("scanned")
                    block = ph.enter_context(nc.Block())
                    K = 5

                    @block.gpsimd
                    def _(g):
                        g.iota(rel[:, :], pattern=[[1, R]], base=0, channel_multiplier=0).then_inc(s_c, 1)

                    @block.sync
                    def _(sp):
                        def load(b, xs, ts):
                            sp.dma_start(X[:, b, :, :].rearrange("p j f -> p (j f)"), rows[:, xs]).then_inc(s_x[b], 16)
                            sp.dma_start(ty[:, b, :], typv[:, ts]).then_inc(s_ty[b], 16)
                        for b in range(2):
                            load(b, slice(b * J * R, (b + 1) * J * R), slice(b * J, (b + 1) * J))
                        with sp.Fori(0, NC // 2 - 1) as i:
                            for b in range(2):
                                sp.wait_ge(s_v, i * (2 * K) + K * (b + 1) + 1)
                                load(b, bass.ds(i * (2 * J * R) + (2 + b) * J * R, J * R), bass.ds(i * (2 * J) + (2 + b) * J, J))

                    @block.vector
                    def _(v):
                        v.wait_ge(s_c, 1)
                        v.sem_inc(s_v, 1)
                        with v.Fori(0, NC // 2) as i:
                            for b in range(2):
                                ch = Chain(v, s_v, i * (2 * K) + K * b + 1)
                                ch.wait()
                                cols = bass.ds(i * (2 * J) + b * J, J)
                                ch(v.tensor_scalar(kp[:, b, :], keep[:, cols], 1.0, None, ALU.mult))
                                v.wait_ge(s_ty[b], i * 16 + 16)
                                ch(v.tensor_tensor(oh[:, :, :], ty[:, b, :].unsqueeze(2).broadcast_to([P, J, R]),
                                                   rel[:, :].unsqueeze(1).broadcast_to([P, J, R]), ALU.is_equal))
                                v.wait_ge(s_x[b], i * 16 + 16)
                                ch.wait()
                                for f in range(R):
                                    v.tensor_tensor_scan(X[:, b, :, f], kp[:, b, :], X[:, b, :, f], first[:, f:f + 1],
                                                         ALU.mult, ALU.add).then_inc(s_scan, 1)
                                v.wait_ge(s_scan, i * (2 * R) + R * (b + 1))
                                ch(v.tensor_copy(first[:, :], X[:, b, J - 1, :]))
                                ch.link(v.tensor_tensor(oh[:, :, :], oh[:, :, :], X[:, b, :, :], ALU.mult))
                                ch(v.reduce_sum(wE[:, cols], oh[:, :, :], axis=AX))
                                assert ch.n == K
                ph.close_block()

        edge_weights()
        with ExitStack() as c:
            sq = sb(c, "sqn2", [P, NT, D])
            m = sb(c, "mn2", [P, NT])
            var = sb(c, "var2", [P, NT])
            Wr1 = sb(c, "Wr1", [D, (R + 1) * D2])
            Wr2 = sb(c, "Wr2", [D2, (R + 1) * D])
            b1n = sb(c, "b1n", [P, D2])
            b2n = sb(c, "b2n2", [P, D])
            root1 = sb(c, "root1", [P, NT, D2])
            root2 = sb(c, "root2", [P, NT, D])
            g32 = sb(c, "g32", [P, NT, D2])
            g16 = sb(c, "g16", [P, NT, D])
            carry32 = sb(c, "carry32", [P, D2])
            carry16 = sb(c, "carry16", [P, D])

            def nothing(v, ch, root, ph):
                pass
            steps("w2", nothing,
                  loads=[(Wr1[:, 0:R * D2].rearrange("d (r f) -> d r f", r=R), L2_W1.rearrange("r d f -> d r f")),
                         (Wr1[:, R * D2:(R + 1) * D2], L2_root1),
                         (Wr2[:, 0:R * D].rearrange("d (r f) -> d r f", r=R), L2_W2.rearrange("r d f -> d r f")),
                         (Wr2[:, R * D:(R + 1) * D], L2_root2),
                         (b1n[:, :], bcast(L2_b1, D2)), (b2n[:, :], bcast(L2_b2, D))])
            with ExitStack() as cc:
                Y1 = sb(cc, "Y1", [P, NT, (R + 1) * D2])
                node_mlp("r1", xN, D, Y1, (R + 1) * D2, Wr1[:, :])

                def keep_root1(v, ch, root, ph):
                    ch.link(v.tensor_tensor(root1[:, :, :], Y1[:, :, R * D2:(R + 1) * D2], over_t(b1n[:, :], D2), ALU.add))
                steps("k1", keep_root1, stores=[(t_rel1.rearrange("(p t r) f -> p t (r f)", p=P, r=R), Y1[:, :, 0:R * D2])])
            sum_pass("q1", t_rel1, D2, relv, S32, carry32, weight=wE)
            collect("d1", S32, D2, carry32, g32)

            def hidden2(v, ch, root, ph):
                ch.link(v.tensor_tensor(g32[:, :, :], g32[:, :, :], over_f(has[:, :], D2), ALU.mult))
                ch.link(v.tensor_tensor(g32[:, :, :], g32[:, :, :], root1[:, :, :], ALU.add))
                ch.link(v.tensor_scalar(g32[:, :, :], g32[:, :, :], 0.0, None, ALU.max))
            steps("h2", hidden2)
            with ExitStack() as cc:
                Y2 = sb(cc, "Y2", [P, NT, (R + 1) * D])
                node_mlp("r2", g32, D2, Y2, (R + 1) * D, Wr2[:, :])

                def keep_root2(v, ch, root, ph):
                    ch.link(v.tensor_tensor(root2[:, :, :], Y2[:, :, R * D:(R + 1) * D], over_t(b2n[:, :], D), ALU.add))
                steps("k2", keep_root2, stores=[(t_rel2.rearrange("(p t r) f -> p t (r f)", p=P, r=R), Y2[:, :, 0:R * D])])
            sum_pass("q2", t_rel2, D, relv, S16, carry16, weight=wE)
            collect("d2", S16, D, carry16, g16)

            def finish2(v, ch, root, ph):
                ch.link(v.tensor_tensor(g16[:, :, :], g16[:, :, :], over_f(has[:, :], D), ALU.mult))
                ch.link(v.tensor_tensor(g16[:, :, :], g16[:, :, :], root2[:, :, :], ALU.add))
                norm_residual(v, ch, root, g16[:, :, :], m[:, :], var[:, :], sq[:, :, :])
            steps("f2", finish2)

        B8 = 8
        NH8 = N // 8

        def sheaf_pass(tag, first, W1q, W2q, b1c, b2n, carry, acc):
            with Phase(tag) as ph:
                C = 2 * D
                ix = ph.sb("ix", [P, 2, J], i32)
                G = ph.sb("G", [P, 2, J, D + 1])
                E1 = ph.sb("E1", [P, 2, J, D + 1])
                h8 = ph.sb("h8", [P, 2, J])
                l8 = ph.sb("l8", [P, 2, J])
                XX = ph.sb("XX", [P, 2, J, C])
                V = ph.sb("V", [P, 2, J, C])
                PR = ph.sb("PR", [P, J, C])
                Y = ph.sb("Y", [P, J, C])
                MS = ph.sb("MS", [P, J, D])
                MD = ph.sb("MD", [P, 2, J, D])
                Mh = ph.sb("Mh", [P, 3, J, D], bf16)
                kp = ph.sb("kp", [P, 2, J])
                n2 = ph.sb("n2", [P, J, 2])
                aa = ph.sb("aa", [P, J, 2])
                dd = ph.sb("dd", [P, J, 2])
                XT = ph.sb("XT", [P, 2, 512])
                PT = ph.sb("PT", [P, 2, 512])
                ihi = ph.sb("ihi", [P, NH8], i32)
                iof = ph.sb("iof", [P, NH8], fp16)
                io8 = ph.sb("io8", [P, 8])
                ohl = ph.sb("ohl", [P, J, 8], bf16)
                lhs = ph.sb("lhs", [P, 2, 3, B8, P], bf16)
                rhs = ph.sb("rhs", [P, 2, B8, NH8], bf16)
                zero = ph.sb("zero", [P, 512], bf16)
                psT = ph.ps("psT", [P, 512])
                psP = [ph.ps(f"psP{q}", [P, 512]) for q in range(2)]
                psV = ph.ps("psV", [P, SUB * C])
                psA = ph.ps("psA", [P, NH8])
                s_ix = [ph.sem(f"index{b}") for b in range(2)]
                s_e1 = [ph.sem(f"dst_rows{b}") for b in range(2)]
                s_k8 = [ph.sem(f"keys{b}") for b in range(2)]
                s_g = [ph.sem(f"gathered{b}") for b in range(2)]
                s_st = [ph.sem(f"stored{b}") for b in range(2)]
                s_c = ph.sem("constants")
                s_xv = ph.sem("spread")
                s_sx = ph.sem("spread_scans")
                s_xx = ph.sem("pairs")
                s_t = ph.sem("transposed")
                s_xt = ph.sem("xt")
                s_m1 = ph.sem("hidden")
                s_h = ph.sem("relu")
                s_m2 = ph.sem("reflections")
                s_vo = ph.sem("reflections_out")
                s_v = ph.sem("vector")
                s_sm = ph.sem("message_scans")
                s_mf = ph.sem("messages_free")
                s_free = ph.sem("slots_free")
                s_b = ph.sem("batch")
                s_sc = ph.sem("scattered")
                s_turn = ph.sem("turn")
                s_acc = ph.sem("sums")
                block = ph.enter_context(nc.Block())
                NS = J // SUB
                NB = J // B8
                KX, KM = 2, 27
                rows = edge_rows(S16)
                xrows = edge_rows(X17)
                F1 = D + 1

                def chunks(eng, body, n):
                    with eng.Fori(0, n // 2) as i:
                        for b in range(2):
                            body(i * 2 + b, b, i)

                @block.sync
                def _(sp):
                    def load(b, c):
                        sp.dma_start(ix[:, b, :], srcv[:, bass.ds(c * J, J)]).then_inc(s_ix[b], 16)
                        sp.dma_start(E1[:, b, :, :].rearrange("p j f -> p (j f)"), xrows[:, bass.ds(c * (J * F1), J * F1)]).then_inc(s_e1[b], 16)
                        sp.dma_start(h8[:, b, :], hi8v[:, bass.ds(c * J, J)]).then_inc(s_k8[b], 16)
                        sp.dma_start(l8[:, b, :], lo8v[:, bass.ds(c * J, J)]).then_inc(s_k8[b], 16)

                    def store(b, c):
                        sp.wait_ge(s_v, c * KM + KM + 1)
                        sp.dma_start(rows[:, bass.ds(c * (J * D), J * D)],
                                     MD[:, b, :, :].rearrange("p j f -> p (j f)")).then_inc(s_st[b], 16)

                    sp.sem_inc(s_free, 2)
                    for b in range(2):
                        load(b, b)

                    def turn(c, b, i):
                        store(b, c)
                        sp.wait_ge(s_st[b], i * 16 + 16)
                        sp.sem_inc(s_free, 1)
                        sp.wait_ge(s_b, c * (11 * NB) + 11 * NB)
                        load(b, c + 2)
                    chunks(sp, turn, NC - 2)
                    for b in range(2):
                        store(b, NC - 2 + b)
                    for b in range(2):
                        sp.wait_ge(s_st[b], 16 * (NC // 2))

                @block.gpsimd
                def _(g):
                    g.iota(ihi[:, :], pattern=[[1, NH8]], base=0, channel_multiplier=0).then_inc(s_c, 1)

                    def gather(i, b):
                        g.wait_ge(s_ix[b], i * 16 + 16)
                        g.wait_ge(s_mf, i * 2 + b + 1)
                        g.sem_inc(s_turn, 1)
                        for j in range(J):
                            g.indirect_dma_start(out=G[:, b, j, :], out_offset=None, in_=t_xdeg,
                                                 in_offset=bass.IndirectOffsetOnAxis(ap=ix[:, b, j:j + 1], axis=0)).then_inc(s_g[b], 16)
                    with g.Fori(0, NC // 2) as i:
                        for b in range(2):
                            gather(i, b)

                @block.scalar
                def _(act):
                    act.sem_inc(s_vo, 1)

                    def turn(i, b):
                        c = i * 2 + b
                        act.wait_ge(s_g[b], i * (16 * J) + 16 * J)
                        act.wait_ge(s_mf, c + 1)
                        act.copy(XX[:, b, :, 0:D], G[:, b, :, 0:D]).then_inc(s_xx, 1)
                        act.wait_ge(s_xv, c * KX + KX + 1)
                        act.copy(XX[:, b, :, D:C], E1[:, b, :, 0:D]).then_inc(s_xx, 1)
                        for s in range(NS):
                            n = c * NS + s
                            act.wait_ge(s_t, n + 1)
                            act.copy(XT[:, s % 2, :], psT[:, :]).then_inc(s_xt, 1)
                            for q in range(4):
                                act.wait_ge(s_m1, n * 4 + q + 1)
                                act.wait_ge(s_m2, n * 4 + q + 1)
                                act.activation(PT[:, q % 2, :], psP[q % 2][:, :], ACT.Relu, bias=b1c).then_inc(s_h, 1)
                            act.wait_ge(s_m2, n * 4 + 6)
                            act.copy(V[:, b, s * SUB:(s + 1) * SUB, :].rearrange("p j f -> p (j f)"), psV[:, :]).then_inc(s_vo, 1)
                    with act.Fori(0, NC // 2) as i:
                        for b in range(2):
                            turn(i, b)

                @block.tensor
                def _(pe):
                    pe.sem_inc(s_m2, 2)
                    pe.sem_inc(s_sc, 2)
                    pe.wait_ge(s_c, 3)
                    for k in range(NH8 // 512):
                        pe.matmul(psA[:, k * 512:(k + 1) * 512], zero[:, 0:P], zero[:, :], start=True, stop=False, skip_group_check=True)

                    def mlp(c, b):
                        pe.wait_ge(s_xx, c * 2 + 2)
                        for s in range(NS):
                            n = c * NS + s
                            for q in range(4):
                                o = s * SUB + 4 * q
                                ins = pe.transpose(psT[:, q * P:(q + 1) * P], XX[:, b, o:o + 4, :].rearrange("p j f -> p (j f)"), ident[:, :])
                            ins.then_inc(s_t, 1)
                            pe.wait_ge(s_xt, n + 1)

                            def first_product(q):
                                pe.matmul(psP[q % 2][:, :], W1q[C * q:C * q + C, :], XT[C * q:C * q + C, s % 2, :],
                                          start=True, stop=True).then_inc(s_m1, 1)

                            def second_product(q):
                                pe.wait_ge(s_h, n * 4 + q + 1)
                                if q == 0:
                                    pe.wait_ge(s_vo, n + 1)
                                for t in range(4):
                                    o = (4 * t + q) * C
                                    ins = pe.matmul(psV[:, o:o + C], PT[:, q % 2, t * P:(t + 1) * P], W2q, start=True, stop=True)
                                ins.then_inc(s_m2, 1)
                            first_product(0)
                            first_product(1)
                            second_product(0)
                            first_product(2)
                            second_product(1)
                            first_product(3)
                            second_product(2)
                            second_product(3)

                    def scatter(c, b):
                        for k in range(NB):
                            pe.wait_ge(s_b, c * (11 * NB) + 11 * (k + 1))
                            for u in range(B8):
                                for part in range(3):
                                    for w in range(NH8 // 512):
                                        ins = pe.matmul(psA[:, w * 512:(w + 1) * 512], lhs[:, k % 2, part, u, :],
                                                        rhs[:, k % 2, u, w * 512:(w + 1) * 512],
                                                        start=False, stop=False, skip_group_check=True)
                            ins.then_inc(s_sc, 1)

                    mlp(0, 0)
                    with pe.Fori(0, NC // 2 - 1) as i:
                        mlp(i * 2 + 1, 1)
                        scatter(i * 2, 0)
                        mlp(i * 2 + 2, 0)
                        scatter(i * 2 + 1, 1)
                    mlp(NC - 1, 1)
                    scatter(NC - 2, 0)
                    scatter(NC - 1, 1)
                    for k in range(NH8 // 512):
                        pe.matmul(psA[:, k * 512:(k + 1) * 512], zero[:, 0:P], zero[:, :], start=False, stop=True,
                                  skip_group_check=True).then_inc(s_acc, 1)

                @block.vector
                def _(v):
                    v.memset(zero[:, :], 0.0).then_inc(s_c, 1)
                    v.memset(carry[:, :], 0.0).then_inc(s_v, 1)
                    v.sem_inc(s_mf, 2)
                    v.sem_inc(s_xv, 1)
                    v.wait_ge(s_c, 2)
                    v.tensor_copy(iof[:, :], ihi[:, :]).then_inc(s_c, 1)
                    v.tensor_copy(io8[:, :], ihi[:, 0:8]).then_inc(s_c, 1)
                    v.wait_ge(s_c, 4)

                    def spread_dst(c, b, i):
                        ch = Chain(v, s_xv, c * KX + 1)
                        ch.wait()
                        ch(v.tensor_scalar(kp[:, b, :], keep[:, bass.ds(c * J, J)], 1.0, None, ALU.mult))
                        v.wait_ge(s_e1[b], i * 16 + 16)
                        ch.wait()
                        for f in range(F1):
                            v.tensor_tensor_scan(E1[:, b, :, f], kp[:, b, :], E1[:, b, :, f], first[:, f:f + 1],
                                                 ALU.mult, ALU.add).then_inc(s_sx, 1)
                        v.wait_ge(s_sx, c * F1 + F1)
                        ch(v.tensor_copy(first[:, :], E1[:, b, J - 1, :]))

                    def pair(t):
                        return t.rearrange("p j (k f) -> p j k f", k=2)

                    def over(t):
                        return t.unsqueeze(3).broadcast_to([P, J, 2, D])

                    def messages(c, b, i):
                        ch = Chain(v, s_v, c * KM + 1)
                        v.wait_ge(s_vo, c * NS + NS + 1)
                        ch.wait()
                        Vb, Xb = V[:, b, :, :], XX[:, b, :, :]
                        tt = v.tensor_tensor
                        ch.link(tt(Vb, Vb, b2n.unsqueeze(1).broadcast_to([P, J, C]), ALU.add))
                        ch.link(tt(PR[:, :, :], Vb, Vb, ALU.mult))
                        ch.link(v.reduce_sum(n2[:, :, :], pair(PR[:, :, :]), axis=AX))
                        ch.link(v.tensor_scalar(n2[:, :, :], n2[:, :, :], 1.0e-24, None, ALU.max))
                        ch.link(v.reciprocal(aa[:, :, :], n2[:, :, :]))
                        ch.link(v.tensor_scalar(aa[:, :, :], aa[:, :, :], 2.0, None, ALU.mult))
                        ch.link(tt(PR[:, :, :], Vb, Xb, ALU.mult))
                        ch.link(v.reduce_sum(dd[:, :, :], pair(PR[:, :, :]), axis=AX))
                        ch.link(tt(dd[:, :, :], dd[:, :, :], aa[:, :, :], ALU.mult))
                        ch.link(tt(pair(PR[:, :, :]), pair(Vb), over(dd[:, :, :]), ALU.mult))
                        ch.link(tt(Y[:, :, :], Xb, PR[:, :, :], ALU.subtract))
                        ch(tt(PR[:, :, 0:D], V[:, b, :, 0:D], Y[:, :, D:C], ALU.mult))
                        ch.link(tt(PR[:, :, D:C], V[:, b, :, D:C], Y[:, :, 0:D], ALU.mult))
                        ch.link(v.reduce_sum(dd[:, :, :], pair(PR[:, :, :]), axis=AX))
                        ch.link(tt(dd[:, :, :], dd[:, :, :], aa[:, :, :], ALU.mult))
                        ch.link(tt(pair(PR[:, :, :]), pair(Vb), over(dd[:, :, :]), ALU.mult))
                        v.wait_ge(s_free, c + 1)
                        ch(tt(MS[:, :, :], Y[:, :, D:C], PR[:, :, 0:D], ALU.subtract))
                        ch.link(tt(MD[:, b, :, :], Y[:, :, 0:D], PR[:, :, D:C], ALU.subtract))
                        ch(tt(MS[:, :, :], MS[:, :, :], E1[:, b, :, D:D + 1].broadcast_to([P, J, D]), ALU.mult))
                        ch.link(tt(MD[:, b, :, :], MD[:, b, :, :], G[:, b, :, D:D + 1].broadcast_to([P, J, D]), ALU.mult))
                        v.sem_inc(s_mf, 1)
                        for f in range(D):
                            v.tensor_tensor_scan(MD[:, b, :, f], kp[:, b, :], MD[:, b, :, f], carry[:, f:f + 1],
                                                 ALU.mult, ALU.add).then_inc(s_sm, 1)
                        ch.link(v.tensor_copy(Mh[:, 0, :, :], MS[:, :, :]))
                        ch.link(tt(MS[:, :, :], MS[:, :, :], Mh[:, 0, :, :], ALU.subtract))
                        ch.link(v.tensor_copy(Mh[:, 1, :, :], MS[:, :, :]))
                        ch.link(tt(MS[:, :, :], MS[:, :, :], Mh[:, 1, :, :], ALU.subtract))
                        ch(v.tensor_copy(Mh[:, 2, :, :], MS[:, :, :]))
                        v.wait_ge(s_k8[b], i * 32 + 32)
                        ch(tt(ohl[:, :, :], l8[:, b, :].unsqueeze(2).broadcast_to([P, J, 8]),
                              io8[:, :].unsqueeze(1).broadcast_to([P, J, 8]), ALU.is_equal))
                        v.wait_ge(s_sm, c * D + D)
                        ch(v.tensor_copy(carry[:, :], MD[:, b, J - 1, :]))
                        ch.wait()
                        assert ch.n == KM, ch.n

                    def build(c, b):
                        for k in range(NB):
                            v.wait_ge(s_sc, c * NB + k + 1)
                            o = k * B8
                            for part in range(3):
                                v.tensor_tensor(lhs[:, k % 2, part, :, :].rearrange("p u (l f) -> p u l f", l=8),
                                                ohl[:, o:o + B8, :].unsqueeze(3).broadcast_to([P, B8, 8, D]),
                                                Mh[:, part, o:o + B8, :].unsqueeze(2).broadcast_to([P, B8, 8, D]),
                                                ALU.mult).then_inc(s_b, 1)
                            for u in range(B8):
                                v.tensor_scalar(rhs[:, k % 2, u, :], iof[:, :], h8[:, b, o + u:o + u + 1], None,
                                                ALU.is_equal).then_inc(s_b, 1)

                    spread_dst(0, 0, 0)
                    with v.Fori(0, NC // 2 - 1) as i:
                        spread_dst(i * 2 + 1, 1, i)
                        messages(i * 2, 0, i)
                        build(i * 2, 0)
                        spread_dst(i * 2 + 2, 0, i + 1)
                        messages(i * 2 + 1, 1, i)
                        build(i * 2 + 1, 1)
                    spread_dst(NC - 1, 1, NC // 2 - 1)
                    messages(NC - 2, 0, NC // 2 - 1)
                    build(NC - 2, 0)
                    messages(NC - 1, 1, NC // 2 - 1)
                    build(NC - 1, 1)
                    v.wait_ge(s_acc, NH8 // 512)
                    v.tensor_copy(acc[:, :], psA[:, :]).then_inc(s_c, 1)
            ph.close_block()

        def unfold_sums(tag, acc):
            with Phase(tag) as ph:
                t = ph.sb("t", [P, NH8])
                psX = ph.ps("psX", [P, NH8])
                s_t = ph.sem("transposed")
                s_c = ph.sem("copied")
                s_st = ph.sem("stored")
                block = ph.enter_context(nc.Block())

                @block.tensor
                def _(pe):
                    for k in range(NH8 // P):
                        pe.transpose(psX[:, k * P:(k + 1) * P], acc[:, k * P:(k + 1) * P], ident[:, :]).then_inc(s_t, 1)

                @block.vector
                def _(v):
                    v.wait_ge(s_t, NH8 // P)
                    v.tensor_copy(t[:, :], psX[:, :]).then_inc(s_c, 1)

                @block.sync
                def _(sp):
                    sp.wait_ge(s_c, 1)
                    sp.dma_start(by_src.rearrange("(k q l) f -> q k (l f)", q=P, l=8),
                                 t[:, :].rearrange("q (k w) -> q k w", w=P)).then_inc(s_st, 16)
                    sp.wait_ge(s_st, 16)
            ph.close_block()

        with ExitStack() as c:
            sq = sb(c, "sqn3", [P, NT, D])
            m = sb(c, "mn3", [P, NT])
            var = sb(c, "var3", [P, NT])
            xd = sb(c, "xd", [P, NT, D + 1])
            first = sb(c, "first17", [P, D + 1])
            W1q = sb(c, "W1q", [P, P])
            W2q = sb(c, "W2q", [P, 2 * D])
            b1c = sb(c, "b1c3", [P, 1])
            b2n = sb(c, "b2n3", [P, 2 * D])
            carry = sb(c, "carry3", [P, D])
            acc = sb(c, "acc", [P, NH8])
            ag = sb(c, "ag3", [P, NT, D])
            bs = sb(c, "bs3", [P, NT, D])

            def table3(v, ch, root, ph):
                ch(v.memset(W2q[:, :], 0.0))
                ch(v.tensor_copy(xd[:, :, 0:D], xN[:, :, :]))
                ch(v.tensor_copy(xd[:, :, D:D + 1], dis3[:, :].unsqueeze(2)))
                ch.wait()
            w1 = []
            for q in range(4):
                r = 2 * D * q
                w1 += [(W1q[r:r + 2 * D, 0:H], L3_W1T),
                       (W1q[r:r + D, H:2 * H], L3_W1T[D:2 * D, :]), (W1q[r + D:r + 2 * D, H:2 * H], L3_W1T[0:D, :])]
            steps("t3", table3, loads=w1 + [(b1c[0:H, :], column(L3_b1)), (b1c[H:2 * H, :], column(L3_b1)),
                                            (b2n[:, 0:D], bcast(L3_b2, D)), (b2n[:, D:2 * D], bcast(L3_b2, D))],
                  stores=[(node_rows(t_xdeg), flat(xd)), (W2q[0:H, 0:D], L3_W2T), (W2q[H:2 * H, D:2 * D], L3_W2T)])
            spread("sp17", xd, X17, t_xdeg, first, D + 1)
            sheaf_pass("sh", first, W1q, W2q[:, :], b1c[:, 0:1], b2n[:, :], carry, acc)
            unfold_sums("us", acc)
            collect("c4", S16, D, carry, ag)

            def finish3(v, ch, root, ph):
                ch.link(v.tensor_tensor(ag[:, :, :], ag[:, :, :], over_f(has[:, :], D), ALU.mult))
                ch.link(v.tensor_tensor(ag[:, :, :], ag[:, :, :], bs[:, :, :], ALU.add))
                ch.link(v.tensor_tensor(ag[:, :, :], ag[:, :, :], over_f(dis3[:, :], D), ALU.mult))
                ch.link(v.tensor_tensor(ag[:, :, :], ag[:, :, :], xN[:, :, :], ALU.add))
                ch.link(v.tensor_scalar(ag[:, :, :], ag[:, :, :], 0.0, None, ALU.max))
                norm_residual(v, ch, root, ag[:, :, :], m[:, :], var[:, :], sq[:, :, :])
            steps("f3", finish3, loads=[(flat(bs), node_rows(by_src))], stores=[(node_rows(out), flat(xN))])


_INS = ["x", "src", "dst", "edge_attr_9", "edge_type_8", "L0_gnn_weights",
        "L0_gnn_W1", "L0_gnn_b1", "L0_gnn_W2", "L0_gnn_b2", "L0_gnn_W3", "L0_gnn_b3", "L0_gnn_W4", "L0_gnn_b4",
        "L1_gnn_W1", "L1_gnn_b1", "L1_gnn_W2", "L1_gnn_b2", "L1_gnn_W3", "L1_gnn_b3",
        "L2_gnn_W1", "L2_gnn_root1", "L2_gnn_b1", "L2_gnn_W2", "L2_gnn_root2", "L2_gnn_b2",
        "L3_gnn_W1", "L3_gnn_b1", "L3_gnn_W2", "L3_gnn_b2"]
_TRANSPOSED = ("L3_gnn_W1", "L3_gnn_W2")


def kernel(**inputs):
    import numpy as _np
    import concourse.bacc as _bacc
    from concourse import mybir as _mybir
    from concourse.bass_utils import run_bass_kernel_spmd as _run

    nc = _bacc.Bacc("TRN2", target_bir_lowering=False, num_devices=1)
    arrays, args = {}, []
    for name in _INS:
        a = _np.asarray(inputs[name])
        a = _np.ascontiguousarray(a.T if name in _TRANSPOSED else a)
        arrays[f"in_{name}"] = a
        args.append(nc.dram_tensor(f"in_{name}", a.shape, _mybir.dt.from_np(a.dtype), kind="ExternalInput").ap())
    args.append(nc.dram_tensor("out_x", inputs["x"].shape, _mybir.dt.float32, kind="ExternalOutput").ap())
    gnn_stack_kernel(nc, *args)
    r = _run(nc, [arrays], core_ids=[0])
    return r.results[0]["out_x"]
```
